# Optimizing a Trainium2 kernel written in Bass

```python
import numpy as np
import jax
import jax.numpy as jnp

def _softmax(x, axis=-1):
    return jax.nn.softmax(x, axis=axis)

def _gelu(x):
    return jax.nn.gelu(x, approximate=True)

def _silu(x):
    return jax.nn.silu(x)

def _sigmoid(x):
    return jax.nn.sigmoid(x)

def _layernorm(x, axis=-1, eps=1e-05):
    m = jnp.mean(x, axis=axis, keepdims=True)
    v = jnp.var(x, axis=axis, keepdims=True)
    return (x - m) / jnp.sqrt(v + eps)

def _scatter_add(tgt, idx, src, axis=0):
    return tgt.at[idx].add(src)

def _segment_sum(src, seg, n):
    return jax.ops.segment_sum(src, seg, n)
kernel_name = 'mk_macaron_d2_jaxref_r8_3030d6'

def setup_inputs(seed: int=0):
    np.random.seed(seed)
    _w = jnp.asarray

    def _L0_attn_setup():
        import jax, jax.numpy as jnp
        import numpy as np
        EPS = 1e-08

        def _l2norm(v):
            return v / (jnp.linalg.norm(v, axis=-1, keepdims=True) + EPS)
        key = jax.random.key(seed)
        k1, k2, k3, k4 = jax.random.split(key, 4)
        B, T, C = (2, 256, 256)
        scale = 1.0 / np.sqrt(C)
        return {'x': jax.random.normal(k1, (B, T, C), dtype=jnp.float32), 'wq': jax.random.normal(k2, (C, C), dtype=jnp.float32) * scale, 'wk': jax.random.normal(k3, (C, C), dtype=jnp.float32) * scale, 'wv': jax.random.normal(k4, (C, C), dtype=jnp.float32) * scale, 'tau': jnp.ones((1,), dtype=jnp.float32), 'nu': jnp.ones((1,), dtype=jnp.float32)}
    _L0_attn_in = _L0_attn_setup()

    def _L0_ffn_setup():
        import jax, jax.numpy as jnp
        import numpy as np
        B, S, H = (4, 128, 256)
        E, K, I, SI = (16, 4, 176, 704)

        def _silu_mul(gu, inter):
            return jax.nn.silu(gu[:, :inter]) * gu[:, inter:]
        key = jax.random.key(seed)
        ks = jax.random.split(key, 7)
        s = 0.02
        return {'hidden_states': jax.random.normal(ks[0], (B, S, H), jnp.float32), 'gate_w': jax.random.normal(ks[1], (E, H), jnp.float32) * s, 'expert_gate_up': jax.random.normal(ks[2], (E, 2 * I, H), jnp.float32) * s, 'expert_down': jax.random.normal(ks[3], (E, H, I), jnp.float32) * s, 'shared_gate_up': jax.random.normal(ks[4], (2 * SI, H), jnp.float32) * s, 'shared_down': jax.random.normal(ks[5], (H, SI), jnp.float32) * s, 'shared_gate_vec': jax.random.normal(ks[6], (1, H), jnp.float32) * s}
    _L0_ffn_in = _L0_ffn_setup()

    def _L1_attn_setup():
        import jax, jax.numpy as jnp
        import numpy as np
        B_, L_, D_MODEL = (2, 512, 256)
        EXPAND, HEADDIM, DCONV = (2, 64, 4)
        INNER = EXPAND * D_MODEL
        NHEADS = INNER // HEADDIM
        key = jax.random.key(seed)
        ks = jax.random.split(key, 8)
        f32 = jnp.float32
        return {'hidden_states': jax.random.normal(ks[0], (B_, L_, D_MODEL), f32), 'in_proj_w': jax.random.normal(ks[1], (INNER, D_MODEL), f32) * 0.02, 'gate_proj_w': jax.random.normal(ks[2], (INNER, D_MODEL), f32) * 0.02, 'out_proj_w': jax.random.normal(ks[3], (D_MODEL, INNER), f32) * 0.02, 'conv_w': jax.random.normal(ks[4], (INNER, DCONV), f32) * 0.02, 'conv_b': jnp.zeros((INNER,), f32), 'dt_w': jax.random.normal(ks[5], (NHEADS, HEADDIM), f32) * 0.02, 'dt_b': jnp.zeros((NHEADS,), f32), 'A_log': jnp.zeros((NHEADS, HEADDIM), f32), 'Bp': jax.random.normal(ks[6], (NHEADS, HEADDIM), f32) * 0.02, 'Cp': jax.random.normal(ks[7], (NHEADS, HEADDIM), f32) * 0.02, 'Dp': jnp.ones((NHEADS, HEADDIM), f32)}
    _L1_attn_in = _L1_attn_setup()

    def _L1_ffn_setup():
        import jax, jax.numpy as jnp
        import numpy as np
        NUM_EXPERTS = 32
        TOP_K = 8
        THRESHOLD = 0.8
        HIDDEN = 256
        INTER = 96
        key = jax.random.key(seed)
        k1, k2, k3, k4 = jax.random.split(key, 4)
        hidden_states = jax.random.normal(k1, (2, 128, HIDDEN), jnp.float32)
        gate_weight = jax.random.normal(k2, (NUM_EXPERTS, HIDDEN), jnp.float32) * 0.02
        gate_up_proj = jax.random.normal(k3, (NUM_EXPERTS, 2 * INTER, HIDDEN), jnp.float32) * 0.02
        down_proj = jax.random.normal(k4, (NUM_EXPERTS, HIDDEN, INTER), jnp.float32) * 0.02
        return {'hidden_states': hidden_states, 'gate_weight': gate_weight, 'gate_up_proj': gate_up_proj, 'down_proj': down_proj}
    _L1_ffn_in = _L1_ffn_setup()
    _d = {'L0_attn_x': _L0_attn_in['x'], 'L0_attn_wq': _L0_attn_in['wq'], 'L0_attn_wk': _L0_attn_in['wk'], 'L0_attn_wv': _L0_attn_in['wv'], 'L0_attn_tau': _L0_attn_in['tau'], 'L0_attn_nu': _L0_attn_in['nu'], 'L0_ffn_gate_w': _L0_ffn_in['gate_w'], 'L0_ffn_expert_gate_up': _L0_ffn_in['expert_gate_up'], 'L0_ffn_expert_down': _L0_ffn_in['expert_down'], 'L0_ffn_shared_gate_up': _L0_ffn_in['shared_gate_up'], 'L0_ffn_shared_down': _L0_ffn_in['shared_down'], 'L0_ffn_shared_gate_vec': _L0_ffn_in['shared_gate_vec'], 'L1_attn_in_proj_w': _L1_attn_in['in_proj_w'], 'L1_attn_gate_proj_w': _L1_attn_in['gate_proj_w'], 'L1_attn_out_proj_w': _L1_attn_in['out_proj_w'], 'L1_attn_conv_w': _L1_attn_in['conv_w'], 'L1_attn_conv_b': _L1_attn_in['conv_b'], 'L1_attn_dt_w': _L1_attn_in['dt_w'], 'L1_attn_dt_b': _L1_attn_in['dt_b'], 'L1_attn_A_log': _L1_attn_in['A_log'], 'L1_attn_Bp': _L1_attn_in['Bp'], 'L1_attn_Cp': _L1_attn_in['Cp'], 'L1_attn_Dp': _L1_attn_in['Dp'], 'L1_ffn_gate_weight': _L1_ffn_in['gate_weight'], 'L1_ffn_gate_up_proj': _L1_ffn_in['gate_up_proj'], 'L1_ffn_down_proj': _L1_ffn_in['down_proj']}
    _x0 = _d['L0_attn_x']
    _d['L0_attn_x'] = jax.random.normal(jax.random.fold_in(jax.random.key(seed), 1), (4, 256, 256), dtype=_x0.dtype)
    del _x0
    return _d

def reference(L0_attn_x, L0_attn_wq, L0_attn_wk, L0_attn_wv, L0_attn_tau, L0_attn_nu, L0_ffn_gate_w, L0_ffn_expert_gate_up, L0_ffn_expert_down, L0_ffn_shared_gate_up, L0_ffn_shared_down, L0_ffn_shared_gate_vec, L1_attn_in_proj_w, L1_attn_gate_proj_w, L1_attn_out_proj_w, L1_attn_conv_w, L1_attn_conv_b, L1_attn_dt_w, L1_attn_dt_b, L1_attn_A_log, L1_attn_Bp, L1_attn_Cp, L1_attn_Dp, L1_ffn_gate_weight, L1_ffn_gate_up_proj, L1_ffn_down_proj):

    def _L0_attn_ref(x, wq, wk, wv, tau, nu):
        import jax, jax.numpy as jnp
        import numpy as np
        EPS = 1e-08

        def _l2norm(v):
            return v / (jnp.linalg.norm(v, axis=-1, keepdims=True) + EPS)
        B, T, C = x.shape
        H = 16
        D = C // H
        q = (x @ wq.T).reshape(B, T, H, D).transpose(0, 2, 1, 3)
        k = (x @ wk.T).reshape(B, T, H, D).transpose(0, 2, 1, 3)
        v = (x @ wv.T).reshape(B, T, H, D).transpose(0, 2, 1, 3)
        q, k, v = (_l2norm(q), _l2norm(k), _l2norm(v))
        scores = jnp.einsum('bhqd,bhkd->bhqk', q, k) * tau[0]
        causal = jnp.tril(jnp.ones((T, T), dtype=bool))
        scores = jnp.where(causal, scores, -jnp.inf)
        p = jax.nn.softmax(scores, axis=-1)
        out = jnp.einsum('bhqk,bhkd->bhqd', p, v)
        out = out.transpose(0, 2, 1, 3).reshape(B, T, C)
        return out * nu[0]

    def _L0_ffn_ref(hidden_states, gate_w, expert_gate_up, expert_down, shared_gate_up, shared_down, shared_gate_vec):
        import jax, jax.numpy as jnp
        import numpy as np
        B, S, H = (4, 128, 256)
        E, K, I, SI = (16, 4, 176, 704)

        def _silu_mul(gu, inter):
            return jax.nn.silu(gu[:, :inter]) * gu[:, inter:]
        orig_shape = hidden_states.shape
        x = hidden_states.reshape(-1, H)
        router_logits = x @ gate_w.T
        routing_probs = jax.nn.softmax(router_logits.astype(jnp.float32), axis=-1)
        topk_w, topk_idx = jax.lax.top_k(routing_probs, K)
        topk_w = topk_w / topk_w.sum(axis=-1, keepdims=True)
        topk_w = topk_w.astype(x.dtype)
        combine = (jax.nn.one_hot(topk_idx, E, dtype=x.dtype) * topk_w[..., None]).sum(1)
        shared = _silu_mul(x @ shared_gate_up.T, SI) @ shared_down.T
        shared = shared * jax.nn.sigmoid(x @ shared_gate_vec.T)

        def step(acc, ew):
            w_gu, w_d, cw = ew
            h = _silu_mul(x @ w_gu.T, I)
            return (acc + h @ w_d.T * cw[:, None], None)
        acc0 = jnp.zeros_like(x)
        sparse, _ = jax.lax.scan(step, acc0, (expert_gate_up, expert_down, combine.T))
        return (shared + sparse).reshape(orig_shape)

    def _L1_attn_ref(hidden_states, in_proj_w, gate_proj_w, out_proj_w, conv_w, conv_b, dt_w, dt_b, A_log, Bp, Cp, Dp):
        import jax, jax.numpy as jnp
        import numpy as np
        B_, L_, D_MODEL = (2, 512, 256)
        EXPAND, HEADDIM, DCONV = (2, 64, 4)
        INNER = EXPAND * D_MODEL
        NHEADS = INNER // HEADDIM
        B, L, _ = hidden_states.shape
        proj = hidden_states @ in_proj_w.T
        gate = jax.nn.sigmoid(hidden_states @ gate_proj_w.T)
        xp = jnp.pad(proj, ((0, 0), (DCONV - 1, 0), (0, 0)))
        conv = conv_b
        for k in range(DCONV):
            conv = conv + xp[:, k:k + L, :] * conv_w[:, k]
        conv = jax.nn.silu(conv)
        X = conv.reshape(B, L, NHEADS, HEADDIM)
        dt = jnp.einsum('blhp,hp->blh', X, dt_w) + dt_b
        dt = jax.nn.softplus(dt)
        A = -jnp.exp(A_log)
        decay = jnp.exp(dt[..., None] * A)
        drive = dt[..., None] * Bp * X

        def step(s, xs):
            d_t, b_t = xs
            s = d_t * s + b_t
            return (s, s)
        s0 = jnp.zeros((B, NHEADS, HEADDIM), X.dtype)
        _, states = jax.lax.scan(step, s0, (jnp.moveaxis(decay, 1, 0), jnp.moveaxis(drive, 1, 0)))
        states = jnp.moveaxis(states, 0, 1)
        y = Cp * states + Dp * X
        combined = y.reshape(B, L, INNER) * gate
        return combined @ out_proj_w.T

    def _L1_ffn_ref(hidden_states, gate_weight, gate_up_proj, down_proj):
        import jax, jax.numpy as jnp
        import numpy as np
        NUM_EXPERTS = 32
        TOP_K = 8
        THRESHOLD = 0.8
        HIDDEN = 256
        INTER = 96
        B, S, H = hidden_states.shape
        x = hidden_states.reshape(-1, H)
        logits = x @ gate_weight.T
        probs = jax.nn.softmax(logits.astype(jnp.float32), axis=-1).astype(logits.dtype)
        top_vals, top_idx = jax.lax.top_k(probs, TOP_K)
        renorm = top_vals / jnp.clip(jnp.sum(top_vals, axis=-1, keepdims=True), 1e-12)
        cum = jnp.cumsum(renorm, axis=-1)
        num_keep = jnp.minimum(jnp.sum((cum < THRESHOLD).astype(jnp.int32), axis=-1) + 1, TOP_K)
        active = jnp.arange(TOP_K)[None, :] < num_keep[:, None]
        rw = top_vals * active.astype(top_vals.dtype)
        rw = rw / jnp.clip(jnp.sum(rw, axis=-1, keepdims=True), 1e-12)
        combine = jnp.sum(jax.nn.one_hot(top_idx, NUM_EXPERTS, dtype=rw.dtype) * rw[..., None], axis=1)

        def body(acc, params):
            w_gu, w_d, ce = params
            gu = x @ w_gu.T
            g, u = jnp.split(gu, 2, axis=-1)
            h = jax.nn.silu(g) * u
            return (acc + h @ w_d.T * ce[:, None], None)
        out, _ = jax.lax.scan(body, jnp.zeros_like(x), (gate_up_proj, down_proj, combine.T))
        return out.reshape(B, S, H)
    x = L0_attn_x
    x = x + 0.5 * _L0_ffn_ref(_layernorm(x, axis=-1), L0_ffn_gate_w, L0_ffn_expert_gate_up, L0_ffn_expert_down, L0_ffn_shared_gate_up, L0_ffn_shared_down, L0_ffn_shared_gate_vec)
    x = x + _L0_attn_ref(_layernorm(x, axis=-1), L0_attn_wq, L0_attn_wk, L0_attn_wv, L0_attn_tau, L0_attn_nu)
    x = x + 0.5 * _L0_ffn_ref(_layernorm(x, axis=-1), L0_ffn_gate_w, L0_ffn_expert_gate_up, L0_ffn_expert_down, L0_ffn_shared_gate_up, L0_ffn_shared_down, L0_ffn_shared_gate_vec)
    x = x + 0.5 * _L1_ffn_ref(_layernorm(x, axis=-1), L1_ffn_gate_weight, L1_ffn_gate_up_proj, L1_ffn_down_proj)
    x = x + _L1_attn_ref(_layernorm(x, axis=-1), L1_attn_in_proj_w, L1_attn_gate_proj_w, L1_attn_out_proj_w, L1_attn_conv_w, L1_attn_conv_b, L1_attn_dt_w, L1_attn_dt_b, L1_attn_A_log, L1_attn_Bp, L1_attn_Cp, L1_attn_Dp)
    x = x + 0.5 * _L1_ffn_ref(_layernorm(x, axis=-1), L1_ffn_gate_weight, L1_ffn_gate_up_proj, L1_ffn_down_proj)
    return x

_drawn_inputs = setup_inputs


def setup_inputs(seed=0):
    import zlib

    import numpy as np

    out = dict(_drawn_inputs(seed))
    spreads = {'L1_attn_conv_b': (0.0, 0.626),
     'L1_attn_dt_b': (0.0, 2.0),
     'L1_attn_A_log': (0.0, 2.0),
     'L1_attn_Dp': (1.0, 0.6)}
    factors = {'L0_attn_wq': 18.686,
     'L0_attn_wk': 6.259,
     'L0_ffn_gate_w': 8.0,
     'L0_ffn_expert_gate_up': 7.877,
     'L0_ffn_expert_down': 7.87,
     'L0_ffn_shared_gate_up': 4.009,
     'L0_ffn_shared_down': 4.005,
     'L0_ffn_shared_gate_vec': 8.0,
     'L1_attn_in_proj_w': 8.0,
     'L1_attn_gate_proj_w': 8.0,
     'L1_attn_out_proj_w': 4.534,
     'L1_attn_conv_w': 8.0,
     'L1_attn_dt_w': 64.0,
     'L1_attn_Bp': 31.081,
     'L1_attn_Cp': 39.433,
     'L1_ffn_gate_weight': 8.0,
     'L1_ffn_gate_up_proj': 8.0,
     'L1_ffn_down_proj': 8.0}
    for name, (base, spread) in spreads.items():
        noise = np.random.default_rng([zlib.crc32(name.encode()), seed]).standard_normal(out[name].shape)
        drawn = base * np.exp(spread * noise) if base else spread * noise
        out[name] = jnp.asarray(drawn.astype(out[name].dtype))
    for name, factor in factors.items():
        out[name] = (out[name] * factor).astype(out[name].dtype)
    return out
```

```python
from contextlib import ExitStack

import concourse.bass as bass
from concourse import mybir

F32 = mybir.dt.float32
F16 = mybir.dt.float16
ALU = mybir.AluOpType
ACT = mybir.ActivationFunctionType
AX = mybir.AxisListType
ds = bass.ds

P = 128
B, T, D = 4, 256, 256
TILES = B * T // P
KC = D // P
HALVES = 2
HT = TILES // HALVES
HN = HT * P
EPS = 1e-5

E0, K0, I0, SI0 = 16, 4, 176, 704
E1, K1, I1 = 32, 8, 96
KEEP = 0.8
EP = 32
PARTS = 3
NCH0 = -(-(E0 * I0 + SI0) // P)
NCH1 = E1 * I1 // P
CW = 2 * KC * P + D
HEADS, HD = 16, 16
INNER, TAPS, SHEADS = 512, 4, 8
CC = INNER // P
WCH0 = NCH0 + KC * 3 * D // CW
WCH1 = NCH1 + (KC * 2 * INNER + CC * D) // CW
SLOTS = 4

NV = TAPS + 5
STAGES = 6

W_SCALE = 256.0
C_SCALE = 4096.0
BIG = 3.0e38

FFN_STAGES = (0, 2, 3, 5)
ATTN_STAGE, SSM_STAGE = 1, 4


def build(nc, x_in, w0_in, w1_in, rw_in, sel0_in, sel1_in, const_in, tau_in, nu_in, vec_in,
          dtw_in, dtb_in, head_in, out, stages=6):
    ctx = ExitStack()
    with ctx:
        def sb(name, shape, dt=F32):
            return ctx.enter_context(nc.sbuf_tensor(name, shape, dt))

        def sem(name):
            return ctx.enter_context(nc.semaphore(name))

        x = sb("x", [P, TILES, D])
        whi = sb("whi", [P, WCH0 * CW], F16)
        wlo = sb("wlo", [P, WCH0 * CW], F16)
        stage = sb("stage", [P, SLOTS, CW])
        sel = sb("sel", [PARTS * EP, NCH0 * P], F16)
        xn = sb("xn", [P, HT, D])
        xhi = sb("xhi", [P, KC, HALVES * HN], F16)
        xlo = sb("xlo", [P, KC, HALVES * HN], F16)
        const = sb("const", [P, 2 * P])
        ident = const[:, 0:P]
        tri = const[:, P:2 * P]
        ident16 = sb("ident16", [P, P], F16)
        zero16 = sb("zero16", [P, P], F16)
        rw = sb("rw", [P, 2 * KC * EP])
        rwhi = sb("rwhi", [P, 2 * KC * EP], F16)
        rwlo = sb("rwlo", [P, 2 * KC * EP], F16)
        half_exp = sb("half_exp", [P, 2, 96])
        stats = sb("stats", [P, HT, 6])
        meanvar = sb("meanvar", [P, HT, 2])
        rstd = sb("rstd", [P, HT])
        logits = sb("logits", [P, HT, EP])
        replaced = sb("replaced", [P, HT, EP])
        picked = sb("picked", [P, HT, EP])
        below = sb("below", [P, HT, EP])
        expd = sb("expd", [P, HT, EP])
        combine = sb("combine", [P, HT, EP])
        top8 = sb("top8", [P, HT, 8])
        to_replace = sb("to_replace", [P, HT, 8])
        below8 = sb("below8", [P, HT, 8])
        exp8 = sb("exp8", [P, HT, 8])
        cum8 = sb("cum8", [P, HT, 8])
        active = sb("active", [P, HT, 8])
        inactive = sb("inactive", [P, HT, 8])
        ones8 = sb("ones8", [P, 8])
        wscale = sb("wscale", [P, 1])
        esum = sb("esum", [P, HT])
        erec = sb("erec", [P, HT])
        sgate = sb("sgate", [P, HT, 1])
        cparts = sb("cparts", [P, HT, PARTS * EP], F16)
        cT = sb("cT", [PARTS * EP, HN], F16)
        gact = sb("gact", [P, 2, HN])
        gfac = sb("gfac", [P, 2, HN])
        hid = sb("hid", [P, 2, HN])
        hhi = sb("hhi", [P, 2, HN], F16)
        hlo = sb("hlo", [P, 2, HN], F16)
        SCR = 48 * 1024 // 4
        scr = sb("scr", [P, SCR])
        at = [0]

        def carve(n32):
            at[0] += n32
            assert at[0] <= SCR, at[0]
            return scr[:, at[0] - n32:at[0]]

        squares = carve(3 * D)
        qkvn = carve(2 * 3 * D).rearrange("p (t c) -> p t c", t=2)
        q4 = carve(2 * HEADS * 64 // 2).bitcast(F16).rearrange("p (t h s d) -> p t h s d", t=2, s=4, d=HD)
        k4 = carve(2 * HEADS * 64 // 2).bitcast(F16).rearrange("p (t h s d) -> p t h s d", t=2, s=4, d=HD)
        q4f = q4.rearrange("p t h s d -> p t (h s d)")
        k4f = k4.rearrange("p t h s d -> p t (h s d)")
        q4T = carve(8 * T // 2).bitcast(F16)
        k4T = carve(8 * T // 2).bitcast(F16)
        VW = 2 * (HD + 1)
        vaug = carve(2 * HEADS * VW // 2).bitcast(F16).rearrange("p (t h c) -> p t h c", t=2, c=VW)
        prob = carve(2 * 768).rearrange("p (b h c) -> p b h c", b=2, h=2)
        phi = carve(768).bitcast(F16).rearrange("p (b h c) -> p b h c", b=2, h=2)
        plo = carve(768).bitcast(F16).rearrange("p (b h c) -> p b h c", b=2, h=2)
        osum = carve(2 * HEADS * VW).rearrange("p (t h c) -> p t h c", t=2, c=VW)
        onum = carve(2 * HEADS * (HD + 1)).rearrange("p (t h c) -> p t h c", t=2, c=HD + 1)
        oout = carve(2 * HEADS * HD).rearrange("p (t h c) -> p t h c", t=2, c=HD)
        ss = sb("ss", [P, 96])
        norm = sb("norm", [P, 96])
        rnorm = sb("rnorm", [P, 96])
        orec = sb("orec", [P, 2 * HEADS])
        tau = sb("tau", [P, 1])
        nu = sb("nu", [P, 1])
        ntau = sb("ntau", [P, 1])
        at[0] = 0
        vec = sb("vec", [P, CC, NV])
        dtw = sb("dtw", [P, CC, SHEADS])
        dtb = sb("dtb", [SHEADS, 1])
        heads = sb("heads", [SHEADS, CC, P])
        nega = sb("nega", [P, CC])
        xs = carve(CC * HN).rearrange("p (c n) -> p c n", c=CC)
        gt = carve(CC * HN).rearrange("p (c n) -> p c n", c=CC)
        xpad = carve(2 * 2 * (T + 3)).rearrange("p (b s n) -> p b s n", b=2, s=2)
        conv = carve(2 * HN).rearrange("p (b n) -> p b n", b=2)
        sp = carve(8 * HN).rearrange("p (b n) -> p b n", b=8)
        at[0] -= 8 * HN
        decay = carve(HN)
        drive = carve(HN)
        states = carve(HN)
        skip = carve(HN)
        comb = carve(HN)
        at[0] += 3 * HN
        chi = carve(2 * HN // 2).bitcast(F16).rearrange("p (b n) -> p b n", b=2)
        clo = carve(2 * HN // 2).bitcast(F16).rearrange("p (b n) -> p b n", b=2)

        ps = ctx.enter_context(nc.psum_tensor("ps", [P, 8, 512], F32))
        F_BANK, G_BANK, U_BANK = (0, 3), (1, 4), (2, 5)
        ACC = 6
        acc = ps[:, ACC:ACC + 2, :].rearrange("p b (t c) -> p (b t) c", c=D)

        x_loaded = [sem(f"x_loaded{h}") for h in range(HALVES)]
        consts_loaded = sem("consts_loaded")
        small_loaded = sem("small_loaded")
        sel_loaded = sem("sel_loaded")
        stage_loaded = [sem(f"stage_loaded{k}") for k in range(SLOTS)]
        out_stored = sem("out_stored")
        pool_consts = sem("pool_consts")
        act_consts = sem("act_consts")
        dve_consts = sem("dve_consts")
        rw_split = sem("rw_split")
        w_scaled = sem("w_scaled")
        w_split = sem("w_split")
        dve_step = sem("dve_step")
        act_step = sem("act_step")
        pool_step = sem("pool_step")
        ln_var = sem("ln_var")
        ln_rstd = sem("ln_rstd")
        ln_xn = sem("ln_xn")
        ln_turned = sem("ln_turned")
        x_hi = sem("x_hi")
        x_lo = sem("x_lo")
        logits_ready = sem("logits_ready")
        exp_in = sem("exp_in")
        exp_out = sem("exp_out")
        cparts_ready = sem("cparts_ready")
        c_turned = sem("c_turned")
        cT_ready = sem("cT_ready")
        gate_ready = sem("gate_ready")
        up_ready = sem("up_ready")
        silu_done = sem("silu_done")
        fac_done = sem("fac_done")
        h_ready = sem("h_ready")
        hi_done = sem("hi_done")
        lo_done = sem("lo_done")
        down_done = sem("down_done")
        x_added = sem("x_added")
        qkv_ready = sem("qkv_ready")
        sq_done = sem("sq_done")
        ss_done = sem("ss_done")
        pow_done = sem("pow_done")
        norm_done = sem("norm_done")
        rnorm_done = sem("rnorm_done")
        qkvn_done = sem("qkvn_done")
        qkv_hi = sem("qkv_hi")
        qkv_lo = sem("qkv_lo")
        qk_turned = sem("qk_turned")
        qT_ready = sem("qT_ready")
        kT_ready = sem("kT_ready")
        s_ready = sem("s_ready")
        p_exp = sem("p_exp")
        p_masked = sem("p_masked")
        p_hi = sem("p_hi")
        p_lo = sem("p_lo")
        pv_done = sem("pv_done")
        o_copied = sem("o_copied")
        o_step = sem("o_step")
        proj_ready = sem("proj_ready")
        sgate_ready = sem("sgate_ready")
        xpad_done = sem("xpad_done")
        tanh_done = sem("tanh_done")
        conv_done = sem("conv_done")
        xs_done = sem("xs_done")
        skip_done = sem("skip_done")
        z_ready = sem("z_ready")
        nabs_done = sem("nabs_done")
        e_done = sem("e_done")
        w_done = sem("w_done")
        ln_done = sem("ln_done")
        dt_done = sem("dt_done")
        dtb_ready = sem("dtb_ready")
        decay_done = sem("decay_done")
        scan_done = sem("scan_done")
        comb_done = sem("comb_done")
        chi_done = sem("chi_done")
        clo_done = sem("clo_done")
        outp_done = sem("outp_done")

        NCH = [NCH0, NCH0, NCH0, NCH0, NCH1, NCH1, NCH1, NCH1]
        BASE = [sum(NCH[:r]) for r in range(8)]

        def steps():
            r = 0
            for s in range(stages):
                if s in FFN_STAGES:
                    for h in range(HALVES):
                        yield "ln", s, h, 2 * s + h
                        yield "route", s, h, r
                        yield "ffn", s, h, r
                        r += 1
                else:
                    for h in range(HALVES):
                        yield "ln", s, h, 2 * s + h
                        yield ("attn" if s == ATTN_STAGE else "ssm"), s, h, h
                if s == 2:
                    yield "weights", s, 0, 1

        def resid(s, h):
            return 2 * s + h + 1 if s < ATTN_STAGE else 2 * s + 2 * h + 2 if s == ATTN_STAGE else 2 * s + h + 3

        def pairs(eng, n, body):
            body(0, True)
            with eng.Fori(1, n // 2) as i:
                body(i, False)

        block = ctx.enter_context(nc.Block())

        @block.sync
        def _(sp):
            xv = x_in.rearrange("(t p) d -> p t d", p=P)
            ov = out.rearrange("(t p) d -> p t d", p=P)
            sp.dma_start(x[:, 0:HT, :], xv[:, 0:HT, :]).then_inc(x_loaded[0], 16)

            def load(src, g, k):
                sp.dma_start(stage[:, k, :], src).then_inc(stage_loaded[k], 16)

            for g in range(SLOTS):
                load(w0_in[g], g, g)
                if g == 0:
                    sp.dma_start(const[:, :], const_in).then_inc(consts_loaded, 16)
                    sp.dma_start(rw[:, :], rw_in).then_inc(consts_loaded, 16)
                    sp.dma_start(sel[:, 0:NCH0 * P], sel0_in).then_inc(sel_loaded, 16)
                    sp.dma_start(x[:, HT:TILES, :], xv[:, HT:TILES, :]).then_inc(x_loaded[1], 16)
            with sp.Fori(1, NCH0 // SLOTS) as i:
                for k in range(SLOTS):
                    sp.wait_ge(w_split, i * SLOTS + (k - SLOTS + 1))
                    load(w0_in[ds(i * SLOTS + k, 1), :, :].rearrange("a p n -> (a p) n"), 0, k)
            for g in range(NCH0, WCH0):
                sp.wait_ge(w_split, g - SLOTS + 1)
                load(w0_in[g], g, g % SLOTS)
            for t, s in ((tau, tau_in), (nu, nu_in)):
                sp.dma_start(t[:, :], s.partition_broadcast(P)).then_inc(small_loaded, 16)
            sp.dma_start(vec[:, :, :], vec_in).then_inc(small_loaded, 16)
            sp.dma_start(dtw[:, :, :], dtw_in).then_inc(small_loaded, 16)
            sp.dma_start(dtb[:, :], dtb_in).then_inc(small_loaded, 16)
            sp.dma_start(heads[:, :, :], head_in).then_inc(small_loaded, 16)
            if stages > 2:
                with sp.Fori(0, WCH1 // SLOTS) as i:
                    for k in range(SLOTS):
                        slot = (WCH0 + k) % SLOTS
                        sp.wait_ge(w_split, i * SLOTS + (WCH0 + k - SLOTS + 1))
                        load(w1_in[ds(i * SLOTS + k, 1), :, :].rearrange("a p n -> (a p) n"), 0, slot)
            if stages > 3:
                sp.wait_ge(down_done, BASE[4])
                sp.dma_start(sel[:, 0:NCH1 * P], sel1_in).then_inc(sel_loaded, 16)
            for h in range(HALVES):
                sp.wait_ge(x_added, resid(stages - 1, h))
                sp.dma_start(ov[:, HT * h:HT * (h + 1), :], x[:, HT * h:HT * (h + 1), :]).then_inc(out_stored, 16)
            sp.wait_ge(small_loaded, 16 * 6)
            sp.wait_ge(out_stored, 32)

        @block.gpsimd
        def _(pool):
            pool.memset(half_exp[:, 0, :], -0.5).then_inc(pool_consts, 1)
            pool.memset(half_exp[:, 1, :], 0.5).then_inc(pool_consts, 1)
            pool.memset(zero16[:, :], 0.0).then_inc(pool_consts, 1)
            pool.memset(combine[:, :, :], 0.0).then_inc(pool_consts, 1)
            pool.memset(ones8[:, :], 1.0).then_inc(pool_consts, 1)
            pool.memset(wscale[:, :], W_SCALE).then_inc(pool_consts, 1)
            pool.wait_ge(consts_loaded, 32)
            pool.tensor_scalar(rwhi[:, :], rw[:, :], W_SCALE, 1.0, ALU.mult, ALU.mult).then_inc(rw_split, 1)
            pool.tensor_scalar(rw[:, :], rw[:, :], W_SCALE, 1.0, ALU.mult, ALU.mult).then_inc(rw_split, 1)
            pool.wait_ge(rw_split, 2)
            pool.tensor_tensor(rwlo[:, :], rw[:, :], rwhi[:, :], ALU.subtract).then_inc(rw_split, 1)

            def split(c, g, k):
                up = wscale[:, :].to_broadcast([P, CW])
                pool.tensor_tensor(whi[:, ds(c * CW, CW)], stage[:, k, :], up, ALU.mult).then_inc(w_scaled, 1)
                pool.tensor_tensor(stage[:, k, :], stage[:, k, :], up, ALU.mult).then_inc(w_scaled, 1)
                pool.wait_ge(w_scaled, g * 2 + 2)
                pool.tensor_tensor(wlo[:, ds(c * CW, CW)], stage[:, k, :], whi[:, ds(c * CW, CW)],
                                   ALU.subtract).then_inc(w_split, 1)

            def ln(n, h):
                pool.wait_ge(pool_consts, 6)
                pool.wait_ge(ln_var, HT * (n + 1))
                pool.tensor_scalar(rstd[:, :], meanvar[:, :, 1], EPS, 1.0, ALU.add, ALU.mult).then_inc(pool_step, 1)
                pool.wait_ge(pool_step, n + 1)
                pool.tensor_tensor(rstd[:, :], rstd[:, :], half_exp[:, 0, 0:HT], ALU.pow).then_inc(ln_rstd, 1)

            def attn(b):
                pool.wait_ge(ss_done, b * 2 + 2)
                pool.tensor_tensor(norm[:, :], ss[:, :], half_exp[:, 1, :], ALU.pow).then_inc(pow_done, 1)
                pool.wait_ge(pow_done, b + 1)
                pool.tensor_scalar(norm[:, :], norm[:, :], 1e-8 * W_SCALE, 1.0, ALU.add, ALU.mult)\
                    .then_inc(norm_done, 1)
                m = tri.unsqueeze(1).unsqueeze(1).to_broadcast([P, 2, 2, P])
                for p in range(8):
                    pool.wait_ge(p_exp, b * 8 + p + 1)
                    diag = prob[:, p % 2, :, :].rearrange("p h (n c) -> p h n c", c=P)[:, :, 0:3:2, :]
                    pool.tensor_tensor(diag, diag, m, ALU.mult).then_inc(p_masked, 1)

            first = True
            for kind, s, h, n in steps():
                if kind == "ln":
                    ln(n, h)
                    if first:
                        first = False
                        with pool.Fori(0, NCH0 // SLOTS) as i:
                            for k in range(SLOTS):
                                pool.wait_ge(stage_loaded[k], i * 16 + 16)
                                split(i * SLOTS + k, i * SLOTS + k, k)
                        for g in range(NCH0, WCH0):
                            pool.wait_ge(stage_loaded[g % SLOTS], 16 * (g // SLOTS + 1))
                            split(g, g, g % SLOTS)
                elif kind == "attn":
                    for b in (2 * h, 2 * h + 1):
                        attn(b)
                elif kind == "weights":
                    with pool.Fori(0, WCH1 // SLOTS) as i:
                        for k in range(SLOTS):
                            slot = (WCH0 + k) % SLOTS
                            pool.wait_ge(stage_loaded[slot], i * 16 + 16 * ((WCH0 + k) // SLOTS + 1))
                            pool.wait_ge(down_done, i * SLOTS + (BASE[3] + k + 1))
                            split(i * SLOTS + k, i * SLOTS + (WCH0 + k), slot)

        @block.scalar
        def _(act):
            act.wait_ge(consts_loaded, 32)
            act.copy(ident16[:, :], ident).then_inc(act_consts, 1)

            def ln(n, h):
                act.wait_ge(ln_turned, HT * (n + 1))
                act.activation(xhi[:, :, HN * h:HN * (h + 1)], ps[:, 0:2, :], ACT.Copy).then_inc(x_hi, 1)

            exps = [0]

            def exp_step(out_ap, in_ap, func, scale=1.0, new=1):
                exps[0] += new
                act.wait_ge(exp_in, exps[0])
                act.activation(out_ap, in_ap, func, scale=scale).then_inc(exp_out, 1)

            def route(r, first_kind):
                if first_kind:
                    exp_step(expd[:, :, 0:E0], below[:, :, 0:E0], ACT.Exp)
                    exp_step(sgate[:, :, :], logits[:, :, E0:E0 + 1], ACT.Tanh, 0.5, new=0)
                else:
                    exp_step(exp8[:, :, :], below8[:, :, :], ACT.Exp)
                    exp_step(expd[:, :, :], below[:, :, :], ACT.Exp)
                act.wait_ge(c_turned, r + 1)
                act.activation(cT[:, :], ps[0:PARTS * EP, 3, 0:HN // 2].bitcast(F16), ACT.Copy)\
                    .then_inc(cT_ready, 1)

            def ffn(r):
                def chunk(c, k, first):
                    act.wait_ge(gate_ready, c + (BASE[r] + 1))
                    if not first:
                        act.wait_ge(fac_done, c + (BASE[r] - 1))
                    act.activation(gact[:, k, :], ps[:, G_BANK[k], :], ACT.Silu, scale=1.0 / W_SCALE)\
                        .then_inc(silu_done, 1)
                    act.wait_ge(h_ready, c + (BASE[r] + 1))
                    if not first:
                        act.wait_ge(down_done, c + (BASE[r] - 1))
                    act.activation(hhi[:, k, :], hid[:, k, :], ACT.Copy).then_inc(hi_done, 1)

                act.preload_act_table(ACT.Silu)
                pairs(act, NCH[r], lambda i, first: [chunk(i * 2 + k, k, first) for k in range(2)])

            def attn(b):
                for t in range(2):
                    act.wait_ge(qkv_ready, b * 2 + t + 1)
                    if b or t:
                        act.wait_ge(ss_done, b * 2 + t)
                    act.activation(squares[:, 0:2 * D], ps[:, 2 * t, :], ACT.Square).then_inc(sq_done, 1)
                    act.activation(squares[:, 2 * D:3 * D], ps[:, 2 * t + 1, 0:D], ACT.Square).then_inc(sq_done, 1)
                for t in range(2):
                    act.wait_ge(qkvn_done, b * 4 + 2 * t + 2)
                    for n, dst in enumerate((q4[:, t, :, 0:2, :], k4[:, t, :, 0:3:2, :])):
                        src = qkvn[:, t, n * D:(n + 1) * D].rearrange("p (h d) -> p h d", d=HD)\
                            .unsqueeze(2).to_broadcast([P, HEADS, 2, HD])
                        act.activation(dst, src, ACT.Copy).then_inc(qkv_hi, 1)
                    if b:
                        act.wait_ge(pv_done, b * 8)
                    act.activation(vaug[:, t, :, 0:HD], qkvn[:, t, 2 * D:3 * D].rearrange("p (h d) -> p h d", d=HD),
                                   ACT.Copy).then_inc(qkv_hi, 1)
                act.wait_ge(qk_turned, b * 2 + 2)
                act.activation(q4T, ps[:, 4:6, :].rearrange("p b n -> p (b n)").bitcast(F16), ACT.Copy)\
                    .then_inc(qT_ready, 1)

                def hi(p):
                    act.wait_ge(p_masked, b * 8 + p + 1)
                    if b or p >= 2:
                        act.wait_ge(pv_done, b * 8 + p - 1)
                    act.activation(phi[:, p % 2, :, :], prob[:, p % 2, :, :], ACT.Copy).then_inc(p_hi, 1)

                for p in range(8):
                    act.wait_ge(s_ready, b * 8 + p + 1)
                    if b or p >= 2:
                        act.wait_ge(p_lo, b * 8 + p - 1)
                    act.activation(prob[:, p % 2, :, :], ps[:, 2 * (p % 3):2 * (p % 3) + 2, 0:384], ACT.Exp,
                                   bias=ntau[:, :], scale=tau[:, :]).then_inc(p_exp, 1)
                    if p:
                        hi(p - 1)
                hi(7)

            def ssm(h):
                def silu(cc):
                    n = CC * h + cc
                    act.wait_ge(conv_done, 4 * n + 4)
                    act.activation(xs[:, cc, :], conv[:, cc % 2, :], ACT.Silu).then_inc(xs_done, 1)

                for cc in range(CC):
                    n = CC * h + cc
                    act.wait_ge(proj_ready, n + 1)
                    if cc >= 2:
                        act.wait_ge(conv_done, 4 * (n - 1))
                    act.activation(xpad[:, cc % 2, :, 3:3 + T],
                                   ps[:, 2 * (cc % 2), :].rearrange("p (s n) -> p s n", s=2),
                                   ACT.Copy, scale=1.0 / W_SCALE).then_inc(xpad_done, 1)
                    act.wait_ge(sgate_ready, n + 1)
                    act.activation(gt[:, cc, :], ps[:, 2 * (cc % 2) + 1, :], ACT.Tanh, scale=0.5 / W_SCALE)\
                        .then_inc(tanh_done, 1)
                    if cc:
                        silu(cc - 1)
                silu(CC - 1)
                act.wait_ge(nabs_done, h + 1)
                act.activation(sp[0:SHEADS, 2, :], sp[0:SHEADS, 1, :], ACT.Exp).then_inc(e_done, 1)
                act.wait_ge(w_done, h + 1)
                act.activation(sp[0:SHEADS, 4, :], sp[0:SHEADS, 3, :], ACT.Ln).then_inc(ln_done, 1)
                for cc in range(CC):
                    n = CC * h + cc
                    act.wait_ge(dtb_ready, n + 1)
                    act.wait_ge(comb_done, n) if cc else act.wait_ge(dt_done, h + 1)
                    act.activation(decay, ps[:, cc % 2, :], ACT.Exp, scale=nega[:, cc:cc + 1]).then_inc(decay_done, 1)
                    act.wait_ge(comb_done, n + 1)
                    if cc >= 2:
                        act.wait_ge(outp_done, n - 1)
                    act.activation(chi[:, cc % 2, :], comb, ACT.Copy).then_inc(chi_done, 1)

            act.wait_ge(consts_loaded, 32)
            setup = False
            for kind, s, h, n in steps():
                if kind == "ln":
                    ln(n, h)
                elif kind == "route":
                    route(n, s < 3)
                elif kind == "ffn":
                    ffn(n)
                elif kind == "attn":
                    if not setup:
                        setup = True
                        act.wait_ge(small_loaded, 16 * 6)
                        act.activation(nega[:, :], vec[:, :, 5], ACT.Exp).then_inc(act_consts, 1)
                        act.wait_ge(dve_consts, 1)
                    for b in (2 * h, 2 * h + 1):
                        attn(b)
                elif kind == "ssm":
                    ssm(h)

        @block.tensor
        def _(pe):
            pe.wait_ge(consts_loaded, 32)
            pe.wait_ge(act_consts, 1)
            pe.wait_ge(pool_consts, 6)
            pe.wait_ge(rw_split, 3)

            def ln(s, n, h):
                if s:
                    pe.wait_ge(x_added, resid(s - 1, h))
                if n:
                    pe.wait_ge(x_lo, n)
                for i in range(HT):
                    pe.wait_ge(ln_xn, HT * n + i + 1)
                    for kc in range(KC):
                        mm = pe.transpose(ps[:, kc, i * P:(i + 1) * P], xn[:, i, kc * P:(kc + 1) * P], ident)
                    mm.then_inc(ln_turned, 1)

            def route(r, h, kind):
                pe.wait_ge(x_hi, lnof(r) + 1)
                pe.wait_ge(x_lo, lnof(r) + 1)
                for i in range(HT):
                    t = HN * h + i * P
                    k = 0
                    for kc in range(KC):
                        w = (kind * KC + kc) * EP
                        for a in (xhi, xlo):
                            for b in (rwhi, rwlo):
                                mm = pe.matmul(ps[:, 2, i * EP:(i + 1) * EP], a[:, kc, t:t + P], b[:, w:w + EP],
                                               start=(k == 0), stop=(k == 7))
                                k += 1
                mm.then_inc(logits_ready, 1)
                pe.wait_ge(cparts_ready, 3 * (r + 1))
                for i in range(HT):
                    mm = pe.transpose(ps[0:PARTS * EP, 3, i * P // 2:(i + 1) * P // 2].bitcast(F16),
                                      cparts[:, i, :], ident16[:, :])
                mm.then_inc(c_turned, 1)

            def lnof(r):
                return 2 * FFN_STAGES[r // 2] + r % 2

            def ffn(r, h):
                t0 = HN * h
                first_use = r in (0, 4)
                base = BASE[r]
                wbase = WCH0 if r >= 4 else 0
                pe.wait_ge(cT_ready, r + 1)
                pe.wait_ge(sel_loaded, 16 if r < 4 else 32)

                def up(c, k):
                    if first_use:
                        pe.wait_ge(w_split, c + (wbase + 1))
                    pe.matmul(ps[:, F_BANK[k], :], sel[:, ds(c * P, P)], cT[:, :], start=True, stop=True)
                    for part, bank, done in ((0, G_BANK[k], gate_ready), (1, U_BANK[k], up_ready)):
                        n = 0
                        for kc in range(KC):
                            off = c * CW + (part * KC + kc) * P
                            for w, a in ((whi, xhi), (whi, xlo), (wlo, xhi)):
                                mm = pe.matmul(ps[:, bank, :], w[:, ds(off, P)], a[:, kc, t0:t0 + HN],
                                               start=(n == 0), stop=(n == 3 * KC - 1))
                                n += 1
                        mm.then_inc(done, 1)

                def down(c, k, last=False):
                    pe.wait_ge(lo_done, c + (base + 1))
                    off = c * CW + 2 * KC * P
                    for i in range(HT):
                        for a, w in ((hhi, whi), (hhi, wlo), (hlo, whi)):
                            mm = pe.matmul(acc[:, i, :], a[:, k, i * P:(i + 1) * P], w[:, ds(off, D)],
                                           start=False, stop=last, skip_group_check=True)
                    mm.then_inc(down_done, 1)

                for b in range(2):
                    pe.matmul(ps[:, ACC + b, :], zero16[:, :], xhi[:, 0, t0:t0 + HN], start=True, stop=False,
                              skip_group_check=True)
                up(0, 0)
                up(1, 1)
                down(0, 0)
                with pe.Fori(1, NCH[r] // 2) as i:
                    pe.wait_ge(h_ready, i * 2 + (base - 1))
                    up(i * 2, 0)
                    down(i * 2 - 1, 1)
                    pe.wait_ge(h_ready, i * 2 + base)
                    up(i * 2 + 1, 1)
                    down(i * 2, 0)
                down(NCH[r] - 1, 1, last=True)

            def attn(b):
                for t in range(2):
                    tok = b * T + t * P
                    for a0, a1, bank in ((0, 2 * D, 2 * t), (2 * D, 3 * D, 2 * t + 1)):
                        n = 0
                        for kc in range(KC):
                            off = NCH0 * CW + kc * 3 * D
                            for a, w in ((xhi, whi), (xhi, wlo), (xlo, whi)):
                                mm = pe.matmul(ps[:, bank, 0:a1 - a0], a[:, kc, tok:tok + P],
                                               w[:, off + a0:off + a1], start=(n == 0), stop=(n == 3 * KC - 1))
                                n += 1
                    mm.then_inc(qkv_ready, 1)
                if b:
                    pe.wait_ge(o_copied, 4 * b)
                for t in range(2):
                    pe.wait_ge(qkv_hi, b * 6 + 3 * t + 3)
                    pe.wait_ge(qkv_lo, b * 6 + 3 * t + 3)
                    for src, bank in ((q4f, 4), (k4f, 6)):
                        for p in range(8):
                            o = (p * T + t * P) // 2
                            dst = ps[:, bank + o // 512, o % 512:o % 512 + P // 2].bitcast(F16)
                            mm = pe.transpose(dst, src[:, t, p * P:(p + 1) * P], ident16[:, :])
                    mm.then_inc(qk_turned, 1)
                pe.wait_ge(qT_ready, b + 1)
                pe.wait_ge(kT_ready, b + 1)

                def scores(p):
                    if p >= 3:
                        pe.wait_ge(p_exp, b * 8 + p - 2)
                    for j in range(2):
                        rows = slice(64 * j, 64 * j + 64)
                        bank = 2 * (p % 3) + j
                        o = p * T
                        pe.matmul(ps[:, bank, 0:T], k4T[rows, o:o + P], q4T[rows, o:o + T], start=True, stop=True)
                        mm = pe.matmul(ps[:, bank, T:T + P], k4T[rows, o + P:o + T], q4T[rows, o + P:o + T],
                                       start=True, stop=True)
                    mm.then_inc(s_ready, 1)

                def pv(p):
                    pe.wait_ge(p_hi, b * 8 + p + 1)
                    pe.wait_ge(p_lo, b * 8 + p + 1)
                    g = p // 2
                    if g >= 2 and p % 2 == 0:
                        pe.wait_ge(o_copied, 4 * b + g - 1)
                    for j in range(2):
                        head = 2 * p + j
                        for qb in range(2):
                            o = (qb * 4 + head % 4) * VW
                            dst = ps[:, 6 + g % 2, o:o + VW]
                            terms = [(a, kb) for kb in range(qb + 1) for a in (phi, plo)]
                            for n, (a, kb) in enumerate(terms):
                                col = qb * P if kb == 0 else T
                                mm = pe.matmul(dst, a[:, p % 2, j, col:col + P], vaug[:, kb, head, :],
                                               start=(n == 0), stop=(n == len(terms) - 1))
                    mm.then_inc(pv_done, 1)

                scores(0)
                scores(1)
                for p in range(8):
                    if p + 2 < 8:
                        scores(p + 2)
                    pv(p)

            def ssm(h):
                t0 = HN * h
                w0 = NCH1 * CW

                def zmm(cc):
                    n = CC * h + cc
                    pe.wait_ge(xs_done, n + 1)
                    mm = pe.matmul(ps[0:SHEADS, 4, :], dtw[:, cc, :], xs[:, cc, :], start=(cc == 0), stop=(cc == CC - 1))
                    if cc == CC - 1:
                        mm.then_inc(z_ready, 1)

                for b in range(2):
                    pe.matmul(ps[:, ACC + b, :], zero16[:, :], xhi[:, 0, t0:t0 + HN], start=True, stop=False,
                              skip_group_check=True)
                for cc in range(CC):
                    n = CC * h + cc
                    if cc >= 2:
                        pe.wait_ge(xpad_done, n - 1)
                        pe.wait_ge(tanh_done, n - 1)
                    for part, done in ((0, proj_ready), (1, sgate_ready)):
                        k = 0
                        for kc in range(KC):
                            off = w0 + kc * 2 * INNER + part * INNER + cc * P
                            for w, a in ((whi, xhi), (whi, xlo), (wlo, xhi)):
                                mm = pe.matmul(ps[:, 2 * (cc % 2) + part, :], w[:, off:off + P], a[:, kc, t0:t0 + HN],
                                               start=(k == 0), stop=(k == 3 * KC - 1))
                                k += 1
                        mm.then_inc(done, 1)
                    if cc:
                        zmm(cc - 1)
                zmm(CC - 1)
                pe.wait_ge(dt_done, h + 1)
                for cc in range(CC):
                    n = CC * h + cc
                    if cc >= 2:
                        pe.wait_ge(scan_done, n - 1)
                    pe.matmul(ps[:, cc % 2, :], heads[:, cc, :], sp[0:SHEADS, 7, :], start=True, stop=True)\
                        .then_inc(dtb_ready, 1)
                    if cc:
                        outp(h, cc - 1)
                outp(h, CC - 1)

            def outp(h, cc):
                n = CC * h + cc
                pe.wait_ge(clo_done, n + 1)
                off = NCH1 * CW + KC * 2 * INNER + cc * D
                for i in range(HT):
                    for a, w in ((chi, whi), (chi, wlo), (clo, whi)):
                        mm = pe.matmul(acc[:, i, :], a[:, cc % 2, i * P:(i + 1) * P], w[:, off:off + D],
                                       start=False, stop=(cc == CC - 1), skip_group_check=True)
                mm.then_inc(outp_done, 1)

            for kind, s, h, n in steps():
                if kind == "ln":
                    ln(s, n, h)
                elif kind == "route":
                    route(n, h, 0 if s < 3 else 1)
                elif kind == "ffn":
                    ffn(n, h)
                elif kind == "attn":
                    pe.wait_ge(x_lo, 2 * s + h + 1)
                    pe.wait_ge(w_split, WCH0)
                    for b in (2 * h, 2 * h + 1):
                        attn(b)
                elif kind == "ssm":
                    pe.wait_ge(x_lo, 2 * s + h + 1)
                    pe.wait_ge(w_split, WCH0 + WCH1)
                    pe.wait_ge(small_loaded, 16 * 6)
                    ssm(h)

        @block.vector
        def _(dve):
            count = [0]

            def step(ins):
                count[0] += 1
                ins.then_inc(dve_step, 1)
                dve.wait_ge(dve_step, count[0])

            def bc(a, n):
                return a.unsqueeze(2).to_broadcast([P, HT, n])

            def ln(s, n, h):
                if s == 0:
                    dve.wait_ge(x_loaded[h], 16)
                else:
                    dve.wait_ge(x_added, resid(s - 1, h))
                for i in range(HT):
                    ins = dve.bn_stats(stats[:, i, :], x[:, HT * h + i, :])
                step(ins)
                for i in range(HT):
                    dve.bn_aggr(meanvar[:, i, :], stats[:, i, :]).then_inc(ln_var, 1)
                dve.wait_ge(ln_var, HT * (n + 1))
                dve.wait_ge(ln_rstd, n + 1)
                if n:
                    dve.wait_ge(ln_turned, HT * n)
                for i in range(HT):
                    dve.tensor_scalar(xn[:, i, :], x[:, HT * h + i, :], meanvar[:, i, 0:1], rstd[:, i:i + 1],
                                      ALU.subtract, ALU.mult).then_inc(ln_xn, 1)
                dve.wait_ge(x_hi, n + 1)
                half = slice(HN * h, HN * (h + 1))
                dve.tensor_tensor(xlo[:, :, half], ps[:, 0:2, :], xhi[:, :, half], ALU.subtract).then_inc(x_lo, 1)

            exps = [0]

            def route(r, first_kind):
                e = E0 if first_kind else E1
                dve.wait_ge(pool_consts, 6)
                dve.wait_ge(logits_ready, r + 1)
                step(dve.tensor_scalar(logits[:, :, :], ps[:, 2, 0:HT * EP].rearrange("p (t e) -> p t e", e=EP),
                                       1.0 / W_SCALE, None, ALU.mult))
                for i in range(HT):
                    ins = dve.max(top8[:, i, :], logits[:, i, 0:e])
                step(ins)
                if first_kind:
                    dve.tensor_tensor(below[:, :, 0:e], logits[:, :, 0:e], top8[:, :, 0:1].to_broadcast([P, HT, e]),
                                      ALU.subtract).then_inc(exp_in, 1)
                    exps[0] += 2
                    dve.tensor_copy(to_replace[:, :, 0:K0], top8[:, :, 0:K0])
                    step(dve.memset(to_replace[:, :, K0:8], BIG))
                else:
                    dve.tensor_tensor(below8[:, :, :], top8[:, :, :], top8[:, :, 0:1].to_broadcast([P, HT, 8]),
                                      ALU.subtract).then_inc(exp_in, 1)
                    dve.tensor_tensor(below[:, :, 0:e], logits[:, :, 0:e], top8[:, :, 0:1].to_broadcast([P, HT, e]),
                                      ALU.subtract).then_inc(exp_in, 1)
                    exps[0] += 2
                    dve.wait_ge(exp_out, exps[0] - 1)
                    step(dve.tensor_reduce(esum[:, :], exp8[:, :, :], AX.X, ALU.add))
                    step(dve.reciprocal(erec[:, :], esum[:, :]))
                    step(dve.tensor_tensor(exp8[:, :, :], exp8[:, :, :], bc(erec[:, :], 8), ALU.mult))
                    dve.memset(active[:, :, 0:1], 1.0)
                    for i in range(HT):
                        ins = dve.tensor_tensor_scan(cum8[:, i, :], ones8[:, :], exp8[:, i, :], 0.0, ALU.mult, ALU.add)
                    step(ins)
                    step(dve.tensor_scalar(active[:, :, 1:8], cum8[:, :, 0:7], KEEP, None, ALU.is_lt))
                    dve.tensor_scalar(inactive[:, :, :], active[:, :, :], -BIG, BIG, ALU.mult, ALU.add)
                    step(dve.tensor_tensor(to_replace[:, :, :], top8[:, :, :], active[:, :, :], ALU.mult))
                    step(dve.tensor_tensor(to_replace[:, :, :], to_replace[:, :, :], inactive[:, :, :], ALU.add))
                for i in range(HT):
                    ins = dve.match_replace(replaced[:, i, 0:e], to_replace[:, i, :], logits[:, i, 0:e], -BIG)
                step(ins)
                step(dve.tensor_tensor(picked[:, :, 0:e], replaced[:, :, 0:e], logits[:, :, 0:e], ALU.not_equal))
                dve.wait_ge(exp_out, exps[0])
                step(dve.tensor_tensor(picked[:, :, 0:e], picked[:, :, 0:e], expd[:, :, 0:e], ALU.mult))
                step(dve.tensor_reduce(esum[:, :], picked[:, :, 0:e], AX.X, ALU.add))
                step(dve.reciprocal(erec[:, :], esum[:, :]))
                step(dve.tensor_scalar(erec[:, :], erec[:, :], C_SCALE, None, ALU.mult))
                if first_kind:
                    dve.tensor_scalar(combine[:, :, E0:E0 + 1], sgate[:, :, :], C_SCALE / 2, C_SCALE / 2,
                                      ALU.mult, ALU.add)
                step(dve.tensor_tensor(combine[:, :, 0:e], picked[:, :, 0:e], bc(erec[:, :], e), ALU.mult))
                for k in range(PARTS):
                    part = cparts[:, :, k * EP:(k + 1) * EP]
                    if r and k == 0:
                        dve.wait_ge(c_turned, r)
                    dve.tensor_copy(part, combine[:, :, :]).then_inc(cparts_ready, 1)
                    dve.wait_ge(cparts_ready, 3 * r + k + 1)
                    if k < PARTS - 1:
                        step(dve.tensor_tensor(combine[:, :, :], combine[:, :, :], part, ALU.subtract))

            def add_to_x(s, h, scale):
                for b in range(2):
                    xb = x[:, HT * h + 2 * b:HT * h + 2 * b + 2, :].rearrange("p t c -> p (t c)")
                    ins = dve.scalar_tensor_tensor(out=xb, in0=ps[:, ACC + b, :], scalar=scale, in1=xb,
                                                   op0=ALU.mult, op1=ALU.add)
                ins.then_inc(x_added, 1)

            def ffn(s, r, h):
                base = BASE[r]

                def chunk(c, k, first):
                    dve.wait_ge(silu_done, c + (base + 1))
                    dve.tensor_tensor(gfac[:, k, :], gact[:, k, :], ps[:, F_BANK[k], :], ALU.mult)\
                        .then_inc(fac_done, 1)
                    dve.wait_ge(fac_done, c + (base + 1))
                    dve.wait_ge(up_ready, c + (base + 1))
                    dve.scalar_tensor_tensor(out=hid[:, k, :], in0=gfac[:, k, :], scalar=1.0 / (W_SCALE * C_SCALE),
                                             in1=ps[:, U_BANK[k], :], op0=ALU.mult, op1=ALU.mult)\
                        .then_inc(h_ready, 1)
                    dve.wait_ge(hi_done, c + (base + 1))
                    if not first:
                        dve.wait_ge(down_done, c + (base - 1))
                    dve.tensor_tensor(hlo[:, k, :], hid[:, k, :], hhi[:, k, :], ALU.subtract).then_inc(lo_done, 1)

                pairs(dve, NCH[r], lambda i, first: [chunk(i * 2 + k, k, first) for k in range(2)])
                dve.wait_ge(down_done, base + NCH[r])
                add_to_x(s, h, 0.5 / W_SCALE)

            def attn(s, b):
                for t in range(2):
                    dve.wait_ge(sq_done, b * 4 + 2 * t + 2)
                    if b or t:
                        pass
                    dve.tensor_reduce(ss[:, 48 * t:48 * t + 48], squares.rearrange("p (h d) -> p h d", d=HD),
                                      AX.X, ALU.add).then_inc(ss_done, 1)
                dve.wait_ge(norm_done, b + 1)
                dve.reciprocal(rnorm[:, :], norm[:, :]).then_inc(rnorm_done, 1)
                dve.wait_ge(rnorm_done, b + 1)
                for t in range(2):
                    for lo, hi, bank in ((0, 32, 2 * t), (32, 48, 2 * t + 1)):
                        dve.tensor_tensor(qkvn[:, t, lo * HD:hi * HD].rearrange("p (h d) -> p h d", d=HD),
                                          ps[:, bank, 0:(hi - lo) * HD].rearrange("p (h d) -> p h d", d=HD),
                                          rnorm[:, 48 * t + lo:48 * t + hi].unsqueeze(2).to_broadcast([P, hi - lo, HD]),
                                          ALU.mult).then_inc(qkvn_done, 1)
                for t in range(2):
                    dve.wait_ge(qkvn_done, b * 4 + 2 * t + 2)
                    dve.wait_ge(qkv_hi, b * 6 + 3 * t + 3)
                    for n, (dst, hi) in enumerate(((q4[:, t, :, 2:4, :], q4[:, t, :, 0:2, :]),
                                                   (k4[:, t, :, 1:4:2, :], k4[:, t, :, 0:3:2, :]))):
                        src = qkvn[:, t, n * D:(n + 1) * D].rearrange("p (h d) -> p h d", d=HD)\
                            .unsqueeze(2).to_broadcast([P, HEADS, 2, HD])
                        dve.tensor_tensor(dst, src, hi, ALU.subtract).then_inc(qkv_lo, 1)
                    dve.tensor_tensor(vaug[:, t, :, HD + 1:2 * HD + 1],
                                      qkvn[:, t, 2 * D:3 * D].rearrange("p (h d) -> p h d", d=HD),
                                      vaug[:, t, :, 0:HD], ALU.subtract).then_inc(qkv_lo, 1)
                dve.wait_ge(qk_turned, b * 2 + 2)
                dve.tensor_copy(k4T, ps[:, 6:8, :].rearrange("p b n -> p (b n)").bitcast(F16)).then_inc(kT_ready, 1)

                def ocopy(g):
                    dve.wait_ge(pv_done, b * 8 + 2 * g + 2)
                    dve.tensor_copy(osum[:, :, 4 * g:4 * g + 4, :],
                                    ps[:, 6 + g % 2, 0:8 * VW].rearrange("p (t h c) -> p t h c", t=2, c=VW))\
                        .then_inc(o_copied, 1)

                for p in range(8):
                    dve.wait_ge(p_hi, b * 8 + p + 1)
                    dve.tensor_tensor(plo[:, p % 2, :, :], prob[:, p % 2, :, :], phi[:, p % 2, :, :], ALU.subtract)\
                        .then_inc(p_lo, 1)
                    if p >= 3 and p % 2:
                        ocopy((p - 3) // 2)
                ocopy(3)
                dve.wait_ge(o_copied, 4 * b + 4)
                dve.tensor_tensor(onum, osum[:, :, :, 0:HD + 1], osum[:, :, :, HD + 1:VW], ALU.add).then_inc(o_step, 1)
                dve.wait_ge(o_step, 4 * b + 1)
                dve.reciprocal(orec[:, :].rearrange("p (t h) -> p t h", t=2), onum[:, :, :, HD]).then_inc(o_step, 1)
                dve.wait_ge(o_step, 4 * b + 2)
                dve.tensor_scalar(orec[:, :], orec[:, :], nu[:, 0:1], None, ALU.mult).then_inc(o_step, 1)
                dve.wait_ge(o_step, 4 * b + 3)
                dve.tensor_tensor(oout, onum[:, :, :, 0:HD],
                                  orec[:, :].rearrange("p (t h) -> p t h", t=2).unsqueeze(3)
                                  .to_broadcast([P, 2, HEADS, HD]), ALU.mult).then_inc(o_step, 1)
                dve.wait_ge(o_step, 4 * b + 4)
                xb = x[:, 2 * b:2 * b + 2, :].rearrange("p t c -> p (t c)")
                dve.tensor_tensor(xb, xb, oout.rearrange("p t h c -> p (t h c)"), ALU.add).then_inc(x_added, 1)

            def ssm(s, h):
                for b in range(2):
                    step(dve.memset(xpad[:, b, :, 0:3], 0.0))
                for cc in range(CC):
                    n = CC * h + cc
                    dve.wait_ge(xpad_done, n + 1)
                    if cc >= 2:
                        dve.wait_ge(xs_done, n - 1)
                    cv = conv[:, cc % 2, :].rearrange("p (s n) -> p s n", s=2)
                    dve.tensor_scalar(cv, xpad[:, cc % 2, :, 0:T], vec[:, cc, 0:1], vec[:, cc, 4:5],
                                      ALU.mult, ALU.add).then_inc(conv_done, 1)
                    for k in range(1, TAPS):
                        dve.wait_ge(conv_done, 4 * n + k)
                        dve.scalar_tensor_tensor(out=cv, in0=xpad[:, cc % 2, :, k:k + T], scalar=vec[:, cc, k:k + 1],
                                                 in1=cv, op0=ALU.mult, op1=ALU.add).then_inc(conv_done, 1)
                z, nabs, e, w, lw, t1, t2, dt = [sp[0:SHEADS, k, :] for k in range(8)]
                dve.wait_ge(z_ready, h + 1)
                step(dve.tensor_scalar(z, ps[0:SHEADS, 4, :], dtb[:, 0:1], None, ALU.add))
                dve.scalar_tensor_tensor(out=nabs, in0=z, scalar=-1.0, in1=z, op0=ALU.mult, op1=ALU.min).then_inc(nabs_done, 1)
                dve.wait_ge(e_done, h + 1)
                dve.tensor_scalar(w, e, 1.0, None, ALU.add).then_inc(w_done, 1)
                dve.tensor_scalar(t2, e, -0.5, 1.0, ALU.mult, ALU.add)
                dve.wait_ge(w_done, h + 1)
                step(dve.scalar_tensor_tensor(out=t1, in0=w, scalar=1.0, in1=e, op0=ALU.subtract, op1=ALU.subtract))
                step(dve.tensor_tensor(t1, t1, t2, ALU.mult))
                dve.wait_ge(ln_done, h + 1)
                step(dve.tensor_tensor(t1, lw, t1, ALU.subtract))
                dve.scalar_tensor_tensor(out=dt, in0=z, scalar=0.0, in1=t1, op0=ALU.max, op1=ALU.add)\
                    .then_inc(dt_done, 1)
                dve.wait_ge(dt_done, h + 1)
                for cc in range(CC):
                    n = CC * h + cc
                    dve.tensor_scalar(skip, xs[:, cc, :], vec[:, cc, 8:9], None, ALU.mult)
                    dve.wait_ge(dtb_ready, n + 1)
                    dve.wait_ge(decay_done, n + 1)
                    step(dve.scalar_tensor_tensor(out=drive, in0=ps[:, cc % 2, :], scalar=vec[:, cc, 6:7],
                                                  in1=xs[:, cc, :], op0=ALU.mult, op1=ALU.mult))
                    for q in range(2):
                        ins = dve.tensor_tensor_scan(states[:, q * T:(q + 1) * T], decay[:, q * T:(q + 1) * T],
                                                     drive[:, q * T:(q + 1) * T], 0.0, ALU.mult, ALU.add)
                    ins.then_inc(scan_done, 1)
                    dve.wait_ge(scan_done, n + 1)
                    step(dve.scalar_tensor_tensor(out=states, in0=states, scalar=vec[:, cc, 7:8], in1=skip,
                                                  op0=ALU.mult, op1=ALU.add))
                    if cc:
                        dve.wait_ge(chi_done, n)
                    dve.scalar_tensor_tensor(out=comb, in0=gt[:, cc, :], scalar=1.0, in1=states,
                                             op0=ALU.add, op1=ALU.mult).then_inc(comb_done, 1)
                    dve.wait_ge(chi_done, n + 1)
                    if cc >= 2:
                        dve.wait_ge(outp_done, n - 1)
                    dve.tensor_tensor(clo[:, cc % 2, :], comb, chi[:, cc % 2, :], ALU.subtract).then_inc(clo_done, 1)
                dve.wait_ge(outp_done, CC * (h + 1))
                add_to_x(s, h, 0.5 / W_SCALE)

            for kind, s, h, n in steps():
                if kind == "ln":
                    ln(s, n, h)
                elif kind == "route":
                    route(n, s < 3)
                elif kind == "ffn":
                    ffn(s, n, h)
                elif kind == "attn":
                    if h == 0:
                        dve.wait_ge(small_loaded, 16 * 6)
                        dve.memset(vaug[:, :, :, HD:HD + 1], 1.0)
                        dve.memset(vaug[:, :, :, VW - 1:VW], 0.0)
                        dve.wait_ge(act_consts, 2)
                        dve.tensor_scalar(nega[:, :], nega[:, :], -1.0, None, ALU.mult)
                        dve.scalar_tensor_tensor(out=ntau[:, :], in0=tau[:, :], scalar=-1.0, in1=tau[:, :],
                                                 op0=ALU.mult, op1=ALU.min)\
                            .then_inc(dve_consts, 1)
                    for b in (2 * h, 2 * h + 1):
                        attn(s, b)
                elif kind == "ssm":
                    ssm(s, h)


def lay_out(i):
    import numpy as np

    f = np.float32
    out = {"x_in": np.ascontiguousarray(i["L0_attn_x"]).reshape(B * T, D)}

    def chunks(gate, up, down, n):
        res = np.zeros((n, P, CW), f)
        for part, w in ((0, gate), (1, up)):
            res[:, :, part * D:(part + 1) * D] = \
                w.reshape(KC, P, n, P).transpose(2, 1, 0, 3).reshape(n, P, KC * P)
        res[:, :, 2 * D:] = down.reshape(n, P, D)
        return res

    def per_partition(w):
        return w.reshape(KC, P, -1).transpose(1, 0, 2).reshape(P, -1, CW).transpose(1, 0, 2)

    gu, dn = i["L0_ffn_expert_gate_up"], i["L0_ffn_expert_down"]
    sgu, sdn = i["L0_ffn_shared_gate_up"], i["L0_ffn_shared_down"]
    gate, up = np.zeros((D, NCH0 * P), f), np.zeros((D, NCH0 * P), f)
    down = np.zeros((NCH0 * P, D), f)
    ne = E0 * I0
    gate[:, :ne] = gu[:, :I0].reshape(ne, D).T
    up[:, :ne] = gu[:, I0:].reshape(ne, D).T
    down[:ne] = dn.transpose(0, 2, 1).reshape(ne, D)
    gate[:, ne:ne + SI0] = sgu[:SI0].T
    up[:, ne:ne + SI0] = sgu[SI0:].T
    down[ne:ne + SI0] = sdn.T
    wqkv = np.concatenate([i["L0_attn_wq"].T, i["L0_attn_wk"].T, i["L0_attn_wv"].T], axis=1)
    out["w0_in"] = np.concatenate([chunks(gate, up, down, NCH0), per_partition(wqkv)])

    gu, dn = i["L1_ffn_gate_up_proj"], i["L1_ffn_down_proj"]
    ne = E1 * I1
    fill = chunks(gu[:, :I1].reshape(ne, D).T, gu[:, I1:].reshape(ne, D).T,
                  dn.transpose(0, 2, 1).reshape(ne, D), NCH1)
    wsg = np.concatenate([i["L1_attn_in_proj_w"].T, i["L1_attn_gate_proj_w"].T], axis=1)
    both = [w.reshape(-1, P, w.shape[1]).transpose(1, 0, 2).reshape(P, -1) for w in (wsg, i["L1_attn_out_proj_w"].T)]
    both = np.concatenate(both, axis=1)
    out["w1_in"] = np.concatenate([fill, both.reshape(P, -1, CW).transpose(1, 0, 2)])

    rw = np.zeros((2, D, EP), f)
    rw[0, :, :E0] = i["L0_ffn_gate_w"].T
    rw[0, :, E0] = i["L0_ffn_shared_gate_vec"][0]
    rw[1, :, :E1] = i["L1_ffn_gate_weight"].T
    out["rw_in"] = np.ascontiguousarray(rw.reshape(2, KC, P, EP).transpose(2, 0, 1, 3).reshape(P, -1))

    row0 = np.arange(NCH0 * P)
    expert0 = np.where(row0 < E0 * I0, row0 // I0, np.where(row0 < E0 * I0 + SI0, E0, -1))
    expert1 = np.arange(NCH1 * P) // I1
    for n, e in ((0, expert0), (1, expert1)):
        out[f"sel{n}_in"] = np.tile(e[None, :] == np.arange(EP)[:, None], (PARTS, 1)).astype(np.float16)
    out["const_in"] = np.concatenate([np.eye(P, dtype=f), np.triu(np.ones((P, P), f))], axis=1)
    out["tau_in"], out["nu_in"] = i["L0_attn_tau"], i["L0_attn_nu"]

    flat = [i["L1_attn_" + k].reshape(INNER) for k in ("conv_b", "A_log", "Bp", "Cp", "Dp")]
    vec = np.concatenate([i["L1_attn_conv_w"], np.stack(flat, axis=1)], axis=1)
    out["vec_in"] = np.ascontiguousarray(vec.reshape(CC, P, NV).transpose(1, 0, 2))
    hd = INNER // SHEADS
    dtw = np.zeros((INNER, SHEADS), f)
    dtw[np.arange(INNER), np.arange(INNER) // hd] = i["L1_attn_dt_w"].reshape(-1)
    out["dtw_in"] = np.ascontiguousarray(dtw.reshape(CC, P, SHEADS).transpose(1, 0, 2))
    out["dtb_in"] = i["L1_attn_dt_b"].reshape(SHEADS, 1)
    out["head_in"] = (np.arange(SHEADS)[:, None] == np.arange(INNER)[None, :] // hd).astype(f).reshape(SHEADS, CC, P)
    return {k: np.ascontiguousarray(v) for k, v in out.items()}


_ORDER = ["x_in", "w0_in", "w1_in", "rw_in", "sel0_in", "sel1_in", "const_in", "tau_in", "nu_in", "vec_in",
          "dtw_in", "dtb_in", "head_in"]


def kernel(**inputs):
    import numpy as _np
    import concourse.bacc as _bacc
    from concourse import mybir as _mybir
    from concourse.bass_utils import run_bass_kernel_spmd as _run

    arrays = lay_out({k: _np.asarray(v) for k, v in inputs.items()})
    nc = _bacc.Bacc("TRN2", target_bir_lowering=False, num_devices=1)
    args = [nc.dram_tensor(n, arrays[n].shape, _mybir.dt.from_np(arrays[n].dtype), kind="ExternalInput").ap()
            for n in _ORDER]
    args.append(nc.dram_tensor("out", (B * T, D), _mybir.dt.float32, kind="ExternalOutput").ap())
    build(nc, *args, stages=STAGES)
    r = _run(nc, [arrays], core_ids=[0])
    return r.results[0]["out"].reshape(B, T, D)
```

```python
from contextlib import ExitStack

import concourse.bass as bass
from concourse import mybir

F32 = mybir.dt.float32
F16 = mybir.dt.float16
I32 = mybir.dt.int32
ALU = mybir.AluOpType
ACT = mybir.ActivationFunctionType
AX = mybir.AxisListType
ds = bass.ds

P = 128
B, T, D = 4, 256, 256
TILES = B * T // P
KC = D // P
HALVES = 2
HT = TILES // HALVES
HN = HT * P
EPS = 1e-5

E0, K0, I0, SI0 = 16, 4, 176, 704
E1, K1, I1 = 32, 8, 96
KEEP = 0.8
EP = 32
PARTS = 3
NCH0 = -(-(E0 * I0 + SI0) // P)
NCH1 = E1 * I1 // P
CW = 2 * KC * P + D
HEADS, HD = 16, 16
INNER, TAPS, SHEADS = 512, 4, 8
CC = INNER // P
WCH0 = NCH0 + KC * 3 * D // CW
WCH1 = NCH1 + (KC * 2 * INNER + CC * D) // CW
SLOTS = 4

NV = TAPS + 5

W_SCALE = 256.0
C_SCALE = 4096.0
BIG = 3.0e38

FFN_STAGES = (0, 2, 3, 5)
ATTN_STAGE, SSM_STAGE = 1, 4
PASSES = len(FFN_STAGES) * HALVES
NCH = [NCH0] * 4 + [NCH1] * 4
BASE = [sum(NCH[:r]) for r in range(PASSES)]
LAG = 2
SEL_CUT = 12
PRE = -1
GAPS = {PRE: 9, 1: 7, 2: 7, 5: 8, 6: 8}


def make_plan():
    plan = {}
    lns = []

    def put(r, c, name, arg, pos="B"):
        plan.setdefault((r, c), []).append((name, arg, pos))

    def ln(s, h, r, c):
        n = len(lns)
        lns.append((s, h))
        put(r, c, "ln_stats", n)
        put(r, c, "ln_pow", n)
        put(r, c + 1, "ln_xn", n)
        put(r, c + 2, "ln_turn", n)
        put(r, c + 3, "ln_hi", n, "A")
        put(r, c + 3, "ln_lo", n)
        return c + 4

    def route(q, r, c):
        put(r, c, "logits", q)
        put(r, c, "route_top", q)
        put(r, c, "route_exp", q)
        if q >= 4:
            c += 1
            put(r, c, "route_keep", q)
        put(r, c + 1, "route_weights", q)
        put(r, c + 2, "route_parts", q)
        put(r, c + 3, "c_turn", q)
        put(r, c + 3, "c_copy", q)

    def attn(h, r):
        for t in range(4):
            n = 4 * h + t
            put(r, 6 + t, "qkv", n)
            put(r, 7 + t, "qkv_copy", n, "A")
            put(r, 7 + t, "qkv_square", n)
            put(r, 8 + t, "qkv_sum", n)
            if t % 2:
                put(r, 9 + t - (t == 3), "qkv_norm", n // 2)
            put(r, 10 + t, "qkv_scale", n)
            put(r, 11 + t, "qkv_hi", n)
            put(r, 11 + t, "k_lo", n)
            put(r, 11 + t, "q_lo", n)
            put(r, 12 + t, "qk_turn", n)
            put(r, 13 + t, "q_copy", n, "A")
            put(r, 13 + t, "k_copy", n)
        for i in range(8):
            n = 16 * h + 2 * i
            c = 17 + i
            put(r, c, "scores", n, "A")
            put(r, c, "p_exp", n)
            put(r, c, "p_lo", n)
            put(r, c, "scores", n + 1)
            put(r, c + 1, "p_exp", n + 1, "A")
            put(r, c + 1, "p_lo", n + 1)
            put(r, c + 2, "pv", n, "A")
            put(r, c + 2, "pv", n + 1, "A")
            put(r, c + 2, "o_copy", n // 2)
            if i % 4 == 3:
                put(r, c + 2, "o_add", 2 * h + i // 4)
        return 26

    def ssm(h, r):
        for cc in range(CC):
            n = CC * h + cc
            put(r, 6 + cc, "proj", n)
            put(r, 8 + cc, "x_tanh", n, "A")
            put(r, 8 + cc, "x_silu", n)
            put(r, 9 + cc, "z", n)
        for cc in range(CC):
            n = CC * h + cc
            put(r, 7 + cc, "x_pad", n, "A")
            put(r, 7 + cc, "g_tanh", n)
            put(r, 7 + cc, "x_conv", n)
        put(r, 13, "sp_arg", h)
        put(r, 13, "sp_exp", h)
        put(r, 14, "sp_one", h)
        put(r, 14, "sp_ln", h)
        put(r, 15, "sp_dt", h)
        put(r, 15, "x_skip", CC * h)
        for cc in range(CC):
            n = CC * h + cc
            put(r, 16 + cc, "dt_spread", n, "A")
            put(r, 16 + cc, "decay", n)
            put(r, 17 + cc, "y", n)
            put(r, 17 + cc, "y_hi", n)
            put(r, 17 + cc, "y_lo", n)
            if cc + 1 < CC:
                put(r, 17 + cc, "x_skip", n + 1)
            put(r, 18 + cc, "out_proj", n)
        for cc in range(CC):
            put(r, 16 + cc, "scan", CC * h + cc)
        put(r, 22, "ssm_add", h)
        return 22

    route(0, PRE, ln(0, 0, PRE, 0))
    route(1, 0, ln(0, 1, 0, 4))
    for h, r in ((0, 1), (1, 2)):
        put(r, 1, "ffn_add", r - 1)
        ln(1, h, r, 2 - (h == 0) * 0)
        c = attn(h, r)
        route(2 + h, r, ln(2, h, r, c))
    put(3, 1, "ffn_add", 2)
    route(4, 3, ln(3, 0, 3, 4))
    put(4, 1, "ffn_add", 3)
    route(5, 4, ln(3, 1, 4, 4))
    for h, r in ((0, 5), (1, 6)):
        put(r, 1, "ffn_add", r - 1)
        ln(4, h, r, 2)
        c = ssm(h, r)
        route(6 + h, r, ln(5, h, r, c))
    put(7, 1, "ffn_add", 6)
    return plan, lns


def build(nc, x_in, w0_in, w1_in, rw_in, sel0_in, sel1_in, const_in, tau_in, nu_in, vec_in,
          dtw_in, dtb_in, head_in, out):
    plan, lns = make_plan()
    ctx = ExitStack()
    with ctx:
        def sb(name, shape, dt=F32):
            return ctx.enter_context(nc.sbuf_tensor(name, shape, dt))

        def sem(name):
            return ctx.enter_context(nc.semaphore(name))

        x = sb("x", [P, TILES, D])
        whi = sb("whi", [P, WCH0 * CW], F16)
        wlo = sb("wlo", [P, WCH0 * CW], F16)
        stage = sb("stage", [P, SLOTS, CW])
        sel = sb("sel", [PARTS * EP, NCH0 * P], F16)
        xn = sb("xn", [P, HT, D])
        xhi = sb("xhi", [P, KC, HALVES * HN], F16)
        xlo = sb("xlo", [P, KC, HALVES * HN], F16)
        const = sb("const", [P, 2 * P])
        ident = const[:, 0:P]
        tri = const[:, P:2 * P]
        ident16 = sb("ident16", [P, P], F16)
        hide16 = sb("hide16", [P, P], F16)
        zero16 = sb("zero16", [P, P], F16)
        rw = sb("rw", [P, 2 * KC * EP])
        rwhi = sb("rwhi", [P, 2 * KC * EP], F16)
        rwlo = sb("rwlo", [P, 2 * KC * EP], F16)
        minus_half = sb("minus_half", [P, HT])
        stats = sb("stats", [P, HT, 6])
        meanvar = sb("meanvar", [P, HT, 2])
        rstd = sb("rstd", [P, HT])
        logits = sb("logits", [P, HT, EP])
        replaced = sb("replaced", [P, HT, EP])
        picked = sb("picked", [P, HT, EP])
        below = sb("below", [P, HT, EP])
        expd = sb("expd", [P, HT, EP])
        combine = sb("combine", [P, HT, EP])
        top8 = sb("top8", [P, HT, 8])
        to_replace = sb("to_replace", [P, HT, 8])
        below8 = sb("below8", [P, HT, 8])
        exp8 = sb("exp8", [P, HT, 8])
        cum8 = sb("cum8", [P, HT, 8])
        active = sb("active", [P, HT, 8])
        inactive = sb("inactive", [P, HT, 8])
        ones8 = sb("ones8", [P, 8])
        esum = sb("esum", [P, HT])
        erec = sb("erec", [P, HT])
        sgate = sb("sgate", [P, HT, 1])
        cparts = sb("cparts", [P, HT, PARTS * EP], F16)
        cT = sb("cT", [PARTS * EP, 2, HN], F16)
        gtanh = sb("gtanh", [P, 2, HN])
        hid = sb("hid", [P, 2, HN])
        hhi = sb("hhi", [P, 4, HN], F16)
        hlo = sb("hlo", [P, 4, HN], F16)
        SCR = 12384
        scr = sb("scr", [P, SCR])
        at = [0]

        def carve(n32):
            at[0] += n32
            assert at[0] <= SCR, at[0]
            return scr[:, at[0] - n32:at[0]]

        VW = 2 * (HD + 1)
        raw01 = carve(2 * 3 * D)
        osum = scr[:, 0:2 * HEADS * VW].rearrange("p (t h c) -> p t h c", t=2, c=VW)
        parts = carve(2 * 2 * HEADS * 64 // 2)
        q4 = parts[:, 0:1024].bitcast(F16).rearrange("p (t h s d) -> p t h s d", t=2, s=4, d=HD)
        k4 = parts[:, 1024:2048].bitcast(F16).rearrange("p (t h s d) -> p t h s d", t=2, s=4, d=HD)
        q4f = q4.rearrange("p t h s d -> p t (h s d)")
        k4f = k4.rearrange("p t h s d -> p t (h s d)")
        q4T = carve(2 * 8 * T // 2).bitcast(F16).rearrange("p (b r n) -> p b r n", b=2, n=T)
        k4T = carve(2 * 8 * T // 2).bitcast(F16).rearrange("p (b r n) -> p b r n", b=2, n=T)
        vaug = carve(4 * HEADS * VW // 2).bitcast(F16).rearrange("p (t h c) -> p t h c", t=4, c=VW)
        prob = carve(2 * 768)
        squares = prob[:, 0:768]
        prob = prob.rearrange("p (b h c) -> p b h c", b=2, h=2)
        more = carve(2 * 768)
        raw = [(raw01 if t < 2 else more)[:, 3 * D * (t % 2):3 * D * (t % 2 + 1)] for t in range(4)]

        def part4(k, off):
            two = (parts if k < 2 else more)[:, off:off + 768].bitcast(F16)
            return two.rearrange("p (b h c) -> p b h c", b=2, h=2)[:, k % 2, :, :]

        phi = [part4(k, 0) for k in range(4)]
        plo = [part4(k, 768) for k in range(4)]
        onum = carve(2 * HEADS * (HD + 1)).rearrange("p (t h c) -> p t h c", t=2, c=HD + 1)
        ss = sb("ss", [P, 2, 48])
        newton = sb("newton", [P, 3, 96])
        rnorm = sb("rnorm", [P, 2, 96])
        orec = sb("orec", [P, 2 * HEADS])
        tau = sb("tau", [P, 1])
        nu = sb("nu", [P, 1])
        ntau = sb("ntau", [P, 1])
        at[0] = 0
        vec = sb("vec", [P, CC, NV])
        dtw = sb("dtw", [P, CC, SHEADS])
        dtb = sb("dtb", [SHEADS, 1])
        nega = sb("nega", [P, CC])
        xs = carve(CC * HN).rearrange("p (c n) -> p c n", c=CC)
        gt = carve(CC * HN).rearrange("p (c n) -> p c n", c=CC)
        xpad = carve(2 * 2 * (T + 3)).rearrange("p (b s n) -> p b s n", b=2, s=2)
        conv = carve(2 * HN).rearrange("p (b n) -> p b n", b=2)
        ctanh = carve(HN)
        sp = carve(8 * HN).rearrange("p (b n) -> p b n", b=8)
        at[0] -= 7 * HN
        decay = carve(HN)
        drive = carve(HN)
        states = carve(HN)
        skip = carve(HN)
        comb = carve(HN)
        chi = carve(2 * HN // 2).bitcast(F16).rearrange("p (b n) -> p b n", b=2)
        clo = carve(2 * HN // 2).bitcast(F16).rearrange("p (b n) -> p b n", b=2)
        heads = carve(CC * P)[0:SHEADS, :].rearrange("p (c n) -> p c n", c=CC)
        DT = 0

        ps = ctx.enter_context(nc.psum_tensor("ps", [P, 8, 512], F32))
        G_BANK, U_BANK, F_BANK, ACC = 0, 1, 2, 3
        S0, S1, S2 = 5, 6, 7
        acc = ps[:, ACC:ACC + 2, :].rearrange("p b (t c) -> p (b t) c", c=D)
        oacc = ps[:, S0:S0 + 2, :].rearrange("p b (t c) -> p (b t) c", c=D)
        flat = ps[:, :, :].rearrange("p b n -> p (b n)")

        x_loaded = [sem(f"x_loaded{h}") for h in range(HALVES)]
        consts_loaded, small_loaded, sel_loaded = sem("consts_loaded"), sem("small_loaded"), sem("sel_loaded")
        stage_loaded = [sem(f"stage_loaded{k}") for k in range(SLOTS)]
        sel1_loaded = [sem(f"sel1_loaded{k}") for k in range(2)]
        out_stored, heads_loaded = sem("out_stored"), sem("heads_loaded")
        pool_consts, act_consts, dve_consts = sem("pool_consts"), sem("act_consts"), sem("dve_consts")
        rw_split, w_scaled, w_split = sem("rw_split"), sem("w_scaled"), sem("w_split")
        dve_step, pool_step = sem("dve_step"), sem("pool_step")
        ln_var, ln_rstd, ln_xn, ln_turned = sem("ln_var"), sem("ln_rstd"), sem("ln_xn"), sem("ln_turned")
        x_hi, x_lo = sem("x_hi"), sem("x_lo")
        logits_ready, exp_in, exp_out = sem("logits_ready"), sem("exp_in"), sem("exp_out")
        cparts_ready, c_turned, cT_ready = sem("cparts_ready"), sem("c_turned"), sem("cT_ready")
        gate_ready, up_ready = sem("gate_ready"), sem("up_ready")
        tanh_done, act_done, fac_done = sem("tanh_done"), sem("act_done"), sem("fac_done")
        h_ready, hi_done, lo_done = sem("h_ready"), sem("hi_done"), sem("lo_done")
        down_done = sem("down_done")
        x_added = [sem(f"x_added{h}") for h in range(HALVES)]
        qkv_ready, raw_done, sq_done, ss_done = sem("qkv_ready"), sem("raw_done"), sem("sq_done"), sem("ss_done")
        rnorm_done, scaled, qkv_his = sem("rnorm_done"), sem("scaled"), sem("qkv_his")
        k_los, q_los, qk_turned = sem("k_los"), sem("q_los"), sem("qk_turned")
        q_copied, k_copied = sem("q_copied"), sem("k_copied")
        s_ready, p_exped, p_his, p_los = sem("s_ready"), sem("p_exped"), sem("p_his"), sem("p_los")
        pv_done, o_copied, o_step = sem("pv_done"), sem("o_copied"), sem("o_step")
        proj_ready, g_ready, xpad_done, tap0_done = sem("proj_ready"), sem("g_ready"), sem("xpad_done"), sem("tap0_done")
        gtanh_done, conv_done, ctanh_done, xs_done = sem("gtanh_done"), sem("conv_done"), sem("ctanh_done"), sem("xs_done")
        skip_done, z_ready, nabs_done, e_done = sem("skip_done"), sem("z_ready"), sem("nabs_done"), sem("e_done")
        one_done, ln_done, dt_done, dt_ready = sem("one_done"), sem("ln_done"), sem("dt_done"), sem("dt_ready")
        decay_done, drive_done, scan_done = sem("decay_done"), sem("drive_done"), sem("scan_done")
        y_done, comb_done, chi_done, clo_done, outp_done = \
            sem("y_done"), sem("comb_done"), sem("chi_done"), sem("clo_done"), sem("outp_done")

        def added(s):
            return s + 1 + (s >= ATTN_STAGE)

        def stage_of(r):
            return FFN_STAGES[r // 2]

        def ln_of(s, h):
            return lns.index((s, h)) + 1

        def run(chunk, piece, down=None):
            waiting = []
            for r in range(PRE, PASSES):
                n = NCH[r] if r >= 0 else 0
                c = 0
                while c < n + GAPS.get(r, 0) or (r == PASSES - 1 and waiting):
                    quiet = 0
                    while c >= 4 and c % 4 == 0 and c + 4 * quiet + 4 <= n and \
                            not any((r, c + 4 * quiet + k) in plan for k in range(4)):
                        quiet += 1
                    if quiet > 1:
                        with chunk.eng.Fori(c // 4, c // 4 + quiet) as i:
                            for k in range(4):
                                chunk(r, i * 4 + k, k, lambda pos: None)
                                if down:
                                    down(r, i * 4 + (k - LAG), (k - LAG) % 4)
                        c += 4 * quiet
                        waiting = [(r, c - 2), (r, c - 1)] if down else []
                        continue

                    def side(pos):
                        for name, arg, where in plan.get((r, c), ()):
                            if where == pos:
                                piece(name, arg)

                    if c < n:
                        chunk(r, c, c % 4, side)
                        waiting.append((r, c))
                    else:
                        side("A")
                    if down and (c >= n or len(waiting) > LAG) and waiting:
                        a, b = waiting.pop(0)
                        down(a, b, b % 4)
                    if not down and c >= n and waiting:
                        waiting.pop(0)
                    if not down and len(waiting) > LAG:
                        waiting.pop(0)
                    side("B")
                    c += 1

        block = ctx.enter_context(nc.Block())

        @block.sync
        def _(sp_):
            xv = x_in.rearrange("(t p) d -> p t d", p=P)
            ov = out.rearrange("(t p) d -> p t d", p=P)
            sp_.dma_start(x[:, 0:HT, :], xv[:, 0:HT, :]).then_inc(x_loaded[0], 16)

            def load(src, k):
                sp_.dma_start(stage[:, k, :], src).then_inc(stage_loaded[k], 16)

            sp_.dma_start(const[:, :], const_in).then_inc(consts_loaded, 16)
            sp_.dma_start(rw[:, :], rw_in).then_inc(consts_loaded, 16)
            for g in range(SLOTS):
                load(w0_in[g], g)
                if g == 0:
                    sp_.dma_start(sel[:, 0:NCH0 * P], sel0_in).then_inc(sel_loaded, 16)
                    sp_.dma_start(x[:, HT:TILES, :], xv[:, HT:TILES, :]).then_inc(x_loaded[1], 16)
            with sp_.Fori(1, NCH0 // SLOTS) as i:
                for k in range(SLOTS):
                    sp_.wait_ge(w_split, i * SLOTS + (k - SLOTS + 1))
                    load(w0_in[ds(i * SLOTS + k, 1), :, :].rearrange("a p n -> (a p) n"), k)
            for g in range(NCH0, WCH0):
                sp_.wait_ge(w_split, g - SLOTS + 1)
                load(w0_in[g], g % SLOTS)
            for t, s in ((tau, tau_in), (nu, nu_in)):
                sp_.dma_start(t[:, :], s.partition_broadcast(P)).then_inc(small_loaded, 16)
            sp_.dma_start(vec[:, :, :], vec_in).then_inc(small_loaded, 16)
            sp_.dma_start(dtw[:, :, :], dtw_in).then_inc(small_loaded, 16)
            sp_.dma_start(dtb[:, :], dtb_in).then_inc(small_loaded, 16)
            with sp_.Fori(0, WCH1 // SLOTS) as i:
                for k in range(SLOTS):
                    sp_.wait_ge(w_split, i * SLOTS + (WCH0 + k - SLOTS + 1))
                    load(w1_in[ds(i * SLOTS + k, 1), :, :].rearrange("a p n -> (a p) n"), (WCH0 + k) % SLOTS)
            for k, (a, b) in enumerate(((0, SEL_CUT), (SEL_CUT, NCH1))):
                sp_.wait_ge(up_ready, BASE[3] + b)
                sp_.dma_start(sel[:, a * P:b * P], sel1_in[:, a * P:b * P]).then_inc(sel1_loaded[k], 16)
            sp_.wait_ge(x_added[1], added(ATTN_STAGE))
            sp_.dma_start(heads, head_in).then_inc(heads_loaded, 16)
            sp_.wait_ge(heads_loaded, 16)
            for h in range(HALVES):
                sp_.wait_ge(x_added[h], added(5))
                sp_.dma_start(ov[:, HT * h:HT * (h + 1), :], x[:, HT * h:HT * (h + 1), :]).then_inc(out_stored, 16)
            sp_.wait_ge(small_loaded, 16 * 5)
            sp_.wait_ge(out_stored, 32)

        SPLIT_AHEAD, SPLIT_BEHIND = 2, 3

        def splits(r, c, k):
            if r == PRE:
                return [(c, c, 0, c)] if c < SPLIT_AHEAD else []
            if r == 0:
                k = k + SPLIT_AHEAD
                return [(c + SPLIT_AHEAD, c + SPLIT_AHEAD, c + (k // 4 * 4 - k + SPLIT_AHEAD), k % 4)]
            if r == 3 and (not isinstance(c, int) or c >= SPLIT_BEHIND):
                k = k - SPLIT_BEHIND + WCH0
                return [(c - SPLIT_BEHIND, c + (WCH0 - SPLIT_BEHIND), c - SPLIT_BEHIND + WCH0 - k % 4, k % 4)]
            if r == 4 and isinstance(c, int) and c < SPLIT_BEHIND + WCH1 - NCH0:
                j = NCH0 - SPLIT_BEHIND + c
                return [(j, WCH0 + j, (WCH0 + j) // 4 * 4, (WCH0 + j) % 4)]
            return []

        @block.gpsimd
        def _(pool):
            pool.memset(minus_half[:, :], -0.5).then_inc(pool_consts, 1)
            pool.memset(zero16[:, :], 0.0).then_inc(pool_consts, 1)
            pool.memset(combine[:, :, :], 0.0).then_inc(pool_consts, 1)
            pool.memset(ones8[:, :], 1.0).then_inc(pool_consts, 1)
            pool.wait_ge(consts_loaded, 32)
            pool.tensor_scalar(rwhi[:, :], rw[:, :], W_SCALE, 1.0, ALU.mult, ALU.mult).then_inc(rw_split, 1)
            pool.tensor_scalar(rw[:, :], rw[:, :], W_SCALE, 1.0, ALU.mult, ALU.mult).then_inc(rw_split, 1)
            pool.wait_ge(rw_split, 2)
            pool.tensor_tensor(rwlo[:, :], rw[:, :], rwhi[:, :], ALU.subtract).then_inc(rw_split, 1)
            pool.wait_ge(pool_consts, 4)

            def split(j, g, k):
                pool.wait_ge(w_scaled, g * 2 + 2)
                pool.tensor_tensor(wlo[:, ds(j * CW, CW)], stage[:, k, :], whi[:, ds(j * CW, CW)],
                                   ALU.subtract).then_inc(w_split, 1)

            def chunk(r, c, k, side):
                pool.wait_ge(hi_done, c + (BASE[r] + 1))
                pool.tensor_tensor(hlo[:, k, :], hid[:, k % 2, :], hhi[:, k, :], ALU.subtract).then_inc(lo_done, 1)
                for j, g, _, slot in splits(r, c, k):
                    split(j, g, slot)
                side("A")

            def piece(name, n):
                if name == "ln_pow":
                    pool.wait_ge(ln_var, HT * (n + 1))
                    pool.tensor_scalar(rstd[:, :], meanvar[:, :, 1], EPS, 1.0, ALU.add, ALU.mult)\
                        .then_inc(pool_step, 1)
                    pool.wait_ge(pool_step, n + 1)
                    pool.tensor_tensor(rstd[:, :], rstd[:, :], minus_half[:, :], ALU.pow).then_inc(ln_rstd, 1)
                elif name == "qkv_square":
                    pool.wait_ge(raw_done, n + 1)
                    if n:
                        pool.wait_ge(ss_done, n)
                    pool.tensor_tensor(squares, raw[n % 4], raw[n % 4], ALU.mult).then_inc(sq_done, 1)
                elif name == "qkv_scale":
                    pool.wait_ge(rnorm_done, n // 2 + 1)
                    v = raw[n % 4].rearrange("p (h d) -> p h d", d=HD)
                    w = rnorm[:, n // 2 % 2, 48 * (n % 2):48 * (n % 2) + 48].unsqueeze(2).to_broadcast([P, 48, HD])
                    pool.tensor_tensor(v, v, w, ALU.mult).then_inc(scaled, 1)
                elif name == "q_lo":
                    pool.wait_ge(qkv_his, n + 1)
                    src = raw[n % 4][:, 0:D].rearrange("p (h d) -> p h d", d=HD)\
                        .unsqueeze(2).to_broadcast([P, HEADS, 2, HD])
                    pool.tensor_tensor(q4[:, n % 2, :, 2:4, :], src, q4[:, n % 2, :, 0:2, :], ALU.subtract)\
                        .then_inc(q_los, 1)
                elif name == "p_lo":
                    pool.wait_ge(p_his, n + 1)
                    pool.tensor_tensor(plo[n % 4], prob[:, n % 2, :, :], phi[n % 4], ALU.subtract).then_inc(p_los, 1)
                elif name == "x_skip":
                    pool.wait_ge(xs_done, n + 1)
                    pool.wait_ge(dt_done, n // CC + 1)
                    if n:
                        pool.wait_ge(y_done, n)
                    pool.wait_ge(dve_consts, 2)
                    pool.tensor_scalar(skip, xs[:, n % CC, :], vec[:, n % CC, 8:9], 1.0, ALU.mult, ALU.mult)\
                        .then_inc(skip_done, 1)
                elif name == "y_lo":
                    pool.wait_ge(chi_done, n + 1)
                    pool.tensor_tensor(clo[:, n % 2, :], comb, chi[:, n % 2, :], ALU.subtract).then_inc(clo_done, 1)
                elif name == "ln_stats" and n == 0:
                    for j in range(SPLIT_AHEAD):
                        split(j, j, j)

            chunk.eng = pool
            run(chunk, piece)

        @block.scalar
        def _(act):
            act.wait_ge(consts_loaded, 32)
            act.copy(ident16[:, :], ident).then_inc(act_consts, 1)

            def chunk(r, c, k, side):
                act.wait_ge(gate_ready, c + (BASE[r] + 1))
                if not (isinstance(c, int) and BASE[r] + c < 2):
                    act.wait_ge(act_done, c + (BASE[r] - 1))
                act.activation(gtanh[:, k % 2, :], ps[:, G_BANK, :], ACT.Tanh, scale=0.5 / W_SCALE)\
                    .then_inc(tanh_done, 1)
                side("A")
                act.wait_ge(h_ready, c + (BASE[r] + 1))
                if not (isinstance(c, int) and BASE[r] + c < 4):
                    act.wait_ge(down_done, c + (BASE[r] - 3))
                act.activation(hhi[:, k, :], hid[:, k % 2, :], ACT.Copy).then_inc(hi_done, 1)

            def piece(name, n):
                if name == "ln_hi":
                    h = lns[n][1]
                    act.wait_ge(ln_turned, HT * (n + 1))
                    act.activation(xhi[:, :, HN * h:HN * (h + 1)], ps[:, S0:S0 + 2, :], ACT.Copy).then_inc(x_hi, 1)
                elif name == "route_exp":
                    args = n if n < 4 else 2 * n - 4
                    act.wait_ge(exp_in, args + 1)
                    if n < 4:
                        act.activation(expd[:, :, 0:E0], below[:, :, 0:E0], ACT.Exp).then_inc(exp_out, 1)
                        act.activation(sgate[:, :, :], logits[:, :, E0:E0 + 1], ACT.Tanh, scale=0.5)\
                            .then_inc(exp_out, 1)
                    else:
                        act.activation(exp8[:, :, :], below8[:, :, :], ACT.Exp).then_inc(exp_out, 1)
                        act.wait_ge(exp_in, args + 2)
                        act.activation(expd[:, :, :], below[:, :, :], ACT.Exp).then_inc(exp_out, 1)
                elif name == "c_copy":
                    act.wait_ge(c_turned, n + 1)
                    act.activation(cT[:, n % 2, :], ps[0:PARTS * EP, S2, 0:HN // 2].bitcast(F16), ACT.Copy)\
                        .then_inc(cT_ready, 1)
                elif name == "qkv_copy":
                    act.wait_ge(qkv_ready, n + 1)
                    if n >= 4:
                        act.wait_ge(x_added[0], added(ATTN_STAGE))
                    act.activation(raw[n % 4], flat[:, S0 * 512:S0 * 512 + 3 * D], ACT.Copy).then_inc(raw_done, 1)
                elif name == "qkv_hi":
                    act.wait_ge(scaled, n + 1)
                    if n >= 2:
                        act.wait_ge(qk_turned, n - 1)
                    for m, dst in enumerate((q4[:, n % 2, :, 0:2, :], k4[:, n % 2, :, 0:3:2, :])):
                        src = raw[n % 4][:, m * D:(m + 1) * D].rearrange("p (h d) -> p h d", d=HD)\
                            .unsqueeze(2).to_broadcast([P, HEADS, 2, HD])
                        act.activation(dst, src, ACT.Copy)
                    act.activation(vaug[:, n % 4, :, 0:HD], raw[n % 4][:, 2 * D:3 * D].rearrange("p (h d) -> p h d", d=HD),
                                   ACT.Copy).then_inc(qkv_his, 1)
                elif name == "q_copy":
                    act.wait_ge(qk_turned, n + 1)
                    act.activation(q4T[:, n // 2 % 2, :, P * (n % 2):P * (n % 2) + P],
                                   ps[:, S0, :].bitcast(F16).rearrange("p (r n) -> p r n", n=P), ACT.Copy)\
                        .then_inc(q_copied, 1)
                elif name == "p_exp":
                    act.wait_ge(s_ready, n + 1)
                    if n == 0:
                        act.wait_ge(dve_consts, 1)
                    if n >= 2:
                        act.wait_ge(p_los, n - 1)
                    act.activation(prob[:, n % 2, :, :], ps[:, S0:S0 + 2, 0:T + P], ACT.Exp, bias=ntau[:, :])\
                        .then_inc(p_exped, 1)
                    act.wait_ge(p_exped, n + 1)
                    if n >= 4:
                        act.wait_ge(pv_done, n - 3)
                    act.activation(phi[n % 4], prob[:, n % 2, :, :], ACT.Copy).then_inc(p_his, 1)
                elif name == "x_pad":
                    act.wait_ge(proj_ready, n + 1)
                    if n >= 2:
                        act.wait_ge(conv_done, 3 * (n - 1))
                        act.wait_ge(xs_done, n - 1)
                    act.wait_ge(dve_consts, 2)
                    act.activation(xpad[:, n % 2, :, 3:3 + T], ps[:, S0, :].rearrange("p (s n) -> p s n", s=2),
                                   ACT.Copy, scale=1.0 / W_SCALE).then_inc(xpad_done, 1)
                    act.wait_ge(xpad_done, n + 1)
                    act.activation(conv[:, n % 2, :].rearrange("p (s n) -> p s n", s=2), xpad[:, n % 2, :, 0:T],
                                   ACT.Identity, bias=vec[:, n % CC, TAPS:TAPS + 1], scale=vec[:, n % CC, 0:1])\
                        .then_inc(tap0_done, 1)
                elif name == "g_tanh":
                    act.wait_ge(g_ready, n + 1)
                    act.activation(gt[:, n % CC, :], ps[:, S1, :], ACT.Tanh, scale=0.5 / W_SCALE).then_inc(gtanh_done, 1)
                elif name == "x_tanh":
                    act.wait_ge(conv_done, 3 * (n + 1))
                    if n:
                        act.wait_ge(xs_done, n)
                    act.activation(ctanh, conv[:, n % 2, :], ACT.Tanh, scale=0.5).then_inc(ctanh_done, 1)
                elif name == "sp_exp":
                    act.wait_ge(nabs_done, n + 1)
                    act.activation(sp[0:SHEADS, 3, :], sp[0:SHEADS, 2, :], ACT.Exp).then_inc(e_done, 1)
                elif name == "sp_ln":
                    act.wait_ge(one_done, n + 1)
                    act.activation(sp[0:SHEADS, 5, :], sp[0:SHEADS, 4, :], ACT.Ln).then_inc(ln_done, 1)
                elif name == "decay":
                    act.wait_ge(dt_ready, n + 1)
                    if n % CC:
                        act.wait_ge(scan_done, n)
                    act.activation(decay, ps[:, S2, :], ACT.Exp, scale=nega[:, n % CC:n % CC + 1]).then_inc(decay_done, 1)
                elif name == "y_hi":
                    act.wait_ge(comb_done, n + 1)
                    if n >= 2:
                        act.wait_ge(outp_done, n - 1)
                    act.activation(chi[:, n % 2, :], comb, ACT.Copy).then_inc(chi_done, 1)
                elif name == "sp_arg" and n == 0:
                    pass
                elif name == "ffn_add" and n == 0:
                    act.wait_ge(small_loaded, 16 * 5)
                    act.activation(nega[:, :], vec[:, :, TAPS + 1], ACT.Exp).then_inc(act_consts, 1)

            chunk.eng = act
            run(chunk, piece)

        @block.tensor
        def _(pe):
            pe.wait_ge(consts_loaded, 32)
            pe.wait_ge(act_consts, 1)
            pe.wait_ge(pool_consts, 4)
            pe.wait_ge(rw_split, 3)

            def chunk(r, c, k, side):
                t0 = HN * (r % 2)
                if isinstance(c, int) and c == 0:
                    pe.wait_ge(x_lo, ln_of(stage_of(r), r % 2))
                    pe.wait_ge(cT_ready, r + 1)
                    if r < 4:
                        pe.wait_ge(sel_loaded, 16)
                    else:
                        for part in sel1_loaded:
                            pe.wait_ge(part, 16)
                if r in (0, 4):
                    pe.wait_ge(w_split, c + ((WCH0 if r else 0) + 1))
                first = isinstance(c, int) and BASE[r] + c == 0
                for part, bank, free in ((0, G_BANK, act_done), (1, U_BANK, h_ready)):
                    if not first:
                        pe.wait_ge(free, c + BASE[r])
                    n = 0
                    for kc in range(KC):
                        off = c * CW + (part * KC + kc) * P
                        for w, a in ((whi, xhi), (whi, xlo), (wlo, xhi)):
                            mm = pe.matmul(ps[:, bank, :], w[:, ds(off, P)], a[:, kc, t0:t0 + HN],
                                           start=(n == 0), stop=(n == 3 * KC - 1))
                            n += 1
                    if part == 0:
                        mm.then_inc(gate_ready, 1)
                side("A")
                pe.matmul(ps[:, F_BANK, :], sel[:, ds(c * P, P)], cT[:, r % 2, :], start=True, stop=True)\
                    .then_inc(up_ready, 1)

            def down(r, c, k):
                if isinstance(c, int) and c == 0:
                    if r:
                        pe.wait_ge(x_added[(r - 1) % 2], added(stage_of(r - 1)))
                    for b in range(2):
                        pe.matmul(ps[:, ACC + b, :], zero16[:, :], xhi[:, 0, 0:HN] if r % 2 == 0 else xhi[:, 0, HN:2 * HN],
                                  start=True, stop=False, skip_group_check=True)
                pe.wait_ge(lo_done, c + (BASE[r] + 1))
                off = c * CW + 2 * KC * P
                last = isinstance(c, int) and c == NCH[r] - 1
                for i in range(HT):
                    for a, w in ((hhi, whi), (hhi, wlo), (hlo, whi)):
                        mm = pe.matmul(acc[:, i, :], a[:, k, i * P:(i + 1) * P], w[:, ds(off, D)],
                                       start=False, stop=last, skip_group_check=True)
                mm.then_inc(down_done, 1)

            def piece(name, n):
                if name == "ln_turn":
                    if n:
                        pe.wait_ge(x_lo, n)
                    for i in range(HT):
                        pe.wait_ge(ln_xn, HT * n + i + 1)
                        for kc in range(KC):
                            mm = pe.transpose(ps[:, S0 + kc, i * P:(i + 1) * P], xn[:, i, kc * P:(kc + 1) * P], ident)
                        mm.then_inc(ln_turned, 1)
                elif name == "logits":
                    h, kind = n % 2, n // 4
                    pe.wait_ge(x_lo, ln_of(stage_of(n), h))
                    if n:
                        pe.wait_ge(cT_ready, n)
                    for i in range(HT):
                        t = HN * h + i * P
                        k = 0
                        for kc in range(KC):
                            w = (kind * KC + kc) * EP
                            for a in (xhi, xlo):
                                for b in (rwhi, rwlo):
                                    mm = pe.matmul(ps[:, S2, i * EP:(i + 1) * EP], a[:, kc, t:t + P], b[:, w:w + EP],
                                                   start=(k == 0), stop=(k == 7))
                                    k += 1
                    mm.then_inc(logits_ready, 1)
                elif name == "c_turn":
                    pe.wait_ge(cparts_ready, 3 * (n + 1))
                    for i in range(HT):
                        mm = pe.transpose(ps[0:PARTS * EP, S2, i * P // 2:(i + 1) * P // 2].bitcast(F16),
                                          cparts[:, i, :], ident16[:, :])
                    mm.then_inc(c_turned, 1)
                elif name == "qkv":
                    pe.wait_ge(x_lo, ln_of(ATTN_STAGE, n // 4))
                    pe.wait_ge(w_split, WCH0)
                    if n:
                        pe.wait_ge(raw_done, n)
                    for a0, a1, bank in ((0, 2 * D, S0), (2 * D, 3 * D, S1)):
                        m = 0
                        for kc in range(KC):
                            off = NCH0 * CW + kc * 3 * D
                            for a, w in ((xhi, whi), (xhi, wlo), (xlo, whi)):
                                mm = pe.matmul(ps[:, bank, 0:a1 - a0], a[:, kc, n * P:n * P + P],
                                               w[:, off + a0:off + a1], start=(m == 0), stop=(m == 3 * KC - 1))
                                m += 1
                    mm.then_inc(qkv_ready, 1)
                elif name == "qk_turn":
                    pe.wait_ge(k_los, n + 1)
                    pe.wait_ge(q_los, n + 1)
                    pe.wait_ge(raw_done, n // 4 * 4 + 4)
                    if n:
                        pe.wait_ge(q_copied, n)
                        pe.wait_ge(k_copied, n)
                    for src, bank in ((q4f, S0), (k4f, S1)):
                        for p in range(8):
                            mm = pe.transpose(ps[:, bank, p * 64:p * 64 + 64].bitcast(F16),
                                              src[:, n % 2, p * P:(p + 1) * P], ident16[:, :])
                    mm.then_inc(qk_turned, 1)
                elif name == "scores":
                    pe.wait_ge(q_copied, n // 16 * 4 + 4)
                    pe.wait_ge(k_copied, n // 16 * 4 + 4)
                    if n:
                        pe.wait_ge(p_exped, n)
                    else:
                        pe.wait_ge(dve_consts, 1)
                    b, p = n // 8 % 2, n % 8
                    for j in range(2):
                        rows = slice(64 * j, 64 * j + 64)
                        pe.matmul(ps[:, S0 + j, 0:T], k4T[rows, b, p, 0:P], q4T[rows, b, p, :], start=True, stop=False,
                                  skip_group_check=True)
                        pe.matmul(ps[:, S0 + j, T:T + P], k4T[rows, b, p, P:T], q4T[rows, b, p, P:T],
                                  start=False, stop=False, skip_group_check=True)
                    for j in range(2):
                        for col in (0, T):
                            mm = pe.matmul(ps[:, S0 + j, col:col + P], ident16[:, :], hide16[:, :],
                                           start=False, stop=True, skip_group_check=True)
                    mm.then_inc(s_ready, 1)
                elif name == "pv":
                    pe.wait_ge(p_los, n + 1)
                    if n % 2 == 0 and n:
                        pe.wait_ge(o_copied, n // 2)
                    b = n // 8 % 2
                    for j in range(2):
                        head = 2 * (n % 8) + j
                        for qb in range(2):
                            o = (qb * 4 + head % 4) * VW
                            terms = [(a, kb) for kb in range(qb + 1) for a in (phi, plo)]
                            for m, (a, kb) in enumerate(terms):
                                col = qb * P if kb == 0 else T
                                mm = pe.matmul(ps[:, S2, o:o + VW], a[n % 4][:, j, col:col + P],
                                               vaug[:, 2 * b + kb, head, :], start=(m == 0), stop=(m == len(terms) - 1))
                    mm.then_inc(pv_done, 1)
                elif name == "proj":
                    h, cc = n // CC, n % CC
                    if cc == 0:
                        pe.wait_ge(x_lo, ln_of(SSM_STAGE, h))
                        pe.wait_ge(w_split, WCH0 + WCH1)
                    else:
                        pe.wait_ge(xpad_done, n)
                        pe.wait_ge(gtanh_done, n)
                    for part, done in ((0, proj_ready), (1, g_ready)):
                        k = 0
                        for kc in range(KC):
                            off = NCH1 * CW + kc * 2 * INNER + part * INNER + cc * P
                            for w, a in ((whi, xhi), (whi, xlo), (wlo, xhi)):
                                mm = pe.matmul(ps[:, S0 + part, :], w[:, off:off + P], a[:, kc, HN * h:HN * (h + 1)],
                                               start=(k == 0), stop=(k == 3 * KC - 1))
                                k += 1
                        mm.then_inc(done, 1)
                elif name == "z":
                    cc = n % CC
                    pe.wait_ge(xs_done, n + 1)
                    pe.wait_ge(small_loaded, 16 * 5)
                    mm = pe.matmul(ps[0:SHEADS, S2, :], dtw[:, cc, :], xs[:, cc, :], start=(cc == 0), stop=(cc == CC - 1))
                    if cc == CC - 1:
                        mm.then_inc(z_ready, 1)
                elif name == "dt_spread":
                    cc = n % CC
                    pe.wait_ge(dt_done, n // CC + 1)
                    pe.wait_ge(heads_loaded, 16)
                    if cc:
                        pe.wait_ge(decay_done, n)
                        pe.wait_ge(drive_done, n)
                    pe.matmul(ps[:, S2, :], heads[:, cc, :], sp[0:SHEADS, DT, :], start=True, stop=True)\
                        .then_inc(dt_ready, 1)
                elif name == "out_proj":
                    cc = n % CC
                    if cc == 0:
                        for b in range(2):
                            pe.matmul(ps[:, S0 + b, :], zero16[:, :], xhi[:, 0, 0:HN], start=True, stop=False,
                                      skip_group_check=True)
                    pe.wait_ge(clo_done, n + 1)
                    off = NCH1 * CW + KC * 2 * INNER + cc * D
                    for i in range(HT):
                        for a, w in ((chi, whi), (chi, wlo), (clo, whi)):
                            mm = pe.matmul(oacc[:, i, :], a[:, n % 2, i * P:(i + 1) * P], w[:, off:off + D],
                                           start=False, stop=(cc == CC - 1), skip_group_check=True)
                    mm.then_inc(outp_done, 1)

            chunk.eng = pe
            run(chunk, piece, down)

        @block.vector
        def _(dve):
            count = [0]

            def step(ins):
                count[0] += 1
                ins.then_inc(dve_step, 1)
                dve.wait_ge(dve_step, count[0])

            def bc(a, n):
                return a.unsqueeze(2).to_broadcast([P, HT, n])

            def split(r, j, g, quarter, k):
                if r == 0 or r == PRE:
                    i = quarter if isinstance(quarter, int) else None
                dve.wait_ge(stage_loaded[k], quarter * 4 + 16)
                if r in (3, 4):
                    dve.wait_ge(down_done, j + (BASE[3] + 1))
                dve.tensor_scalar(whi[:, ds(j * CW, CW)], stage[:, k, :], W_SCALE, None, ALU.mult).then_inc(w_scaled, 1)
                dve.tensor_scalar(stage[:, k, :], stage[:, k, :], W_SCALE, None, ALU.mult).then_inc(w_scaled, 1)

            def chunk(r, c, k, side):
                base = BASE[r]
                a = hid[:, k % 2, :]
                side("A")
                dve.wait_ge(tanh_done, c + (base + 1))
                if not (isinstance(c, int) and base + c < 2):
                    dve.wait_ge(lo_done, c + (base - 1))
                dve.scalar_tensor_tensor(out=a, in0=gtanh[:, k % 2, :], scalar=1.0, in1=ps[:, G_BANK, :],
                                         op0=ALU.add, op1=ALU.mult).then_inc(act_done, 1)
                dve.wait_ge(act_done, c + (base + 1))
                dve.wait_ge(up_ready, c + (base + 1))
                dve.tensor_tensor(a, a, ps[:, F_BANK, :], ALU.mult).then_inc(fac_done, 1)
                dve.wait_ge(fac_done, c + (base + 1))
                dve.scalar_tensor_tensor(out=a, in0=a, scalar=0.5 / (W_SCALE * W_SCALE * C_SCALE), in1=ps[:, U_BANK, :],
                                         op0=ALU.mult, op1=ALU.mult).then_inc(h_ready, 1)
                for j, g, quarter, slot in splits(r, c, k):
                    split(r, j, g, quarter, slot)

            def add_to_x(bank, h, scale):
                for b in range(2):
                    xb = x[:, HT * h + 2 * b:HT * h + 2 * b + 2, :].rearrange("p t c -> p (t c)")
                    ins = dve.scalar_tensor_tensor(out=xb, in0=ps[:, bank + b, :], scalar=scale, in1=xb,
                                                   op0=ALU.mult, op1=ALU.add)
                ins.then_inc(x_added[h], 1)

            def ffn_add(r):
                dve.wait_ge(down_done, BASE[r] + NCH[r])
                add_to_x(ACC, r % 2, 0.5 / W_SCALE)

            def piece(name, n):
                if name == "ln_stats":
                    s, h = lns[n]
                    if n == 0:
                        for j in range(SPLIT_AHEAD):
                            split(PRE, j, j, 0, j)
                    if s == 0:
                        dve.wait_ge(x_loaded[h], 16)
                    else:
                        dve.wait_ge(x_added[h], added(s - 1))
                    for i in range(HT):
                        ins = dve.bn_stats(stats[:, i, :], x[:, HT * h + i, :])
                    step(ins)
                    for i in range(HT):
                        dve.bn_aggr(meanvar[:, i, :], stats[:, i, :]).then_inc(ln_var, 1)
                elif name == "ln_xn":
                    s, h = lns[n]
                    dve.wait_ge(ln_var, HT * (n + 1))
                    dve.wait_ge(ln_rstd, n + 1)
                    if n:
                        dve.wait_ge(ln_turned, HT * n)
                    for i in range(HT):
                        dve.tensor_scalar(xn[:, i, :], x[:, HT * h + i, :], meanvar[:, i, 0:1], rstd[:, i:i + 1],
                                          ALU.subtract, ALU.mult).then_inc(ln_xn, 1)
                elif name == "ln_lo":
                    h = lns[n][1]
                    dve.wait_ge(x_hi, n + 1)
                    half = slice(HN * h, HN * (h + 1))
                    dve.tensor_tensor(xlo[:, :, half], ps[:, S0:S0 + 2, :], xhi[:, :, half], ALU.subtract)\
                        .then_inc(x_lo, 1)
                elif name == "route_top":
                    e = E0 if n < 4 else E1
                    dve.wait_ge(pool_consts, 4)
                    dve.wait_ge(logits_ready, n + 1)
                    step(dve.tensor_scalar(logits[:, :, :], ps[:, S2, 0:HT * EP].rearrange("p (t e) -> p t e", e=EP),
                                           1.0 / W_SCALE, None, ALU.mult))
                    for i in range(HT):
                        ins = dve.max(top8[:, i, :], logits[:, i, 0:e])
                    step(ins)
                    if n >= 4:
                        dve.tensor_tensor(below8[:, :, :], top8[:, :, :], top8[:, :, 0:1].to_broadcast([P, HT, 8]),
                                          ALU.subtract).then_inc(exp_in, 1)
                    dve.tensor_tensor(below[:, :, 0:e], logits[:, :, 0:e], top8[:, :, 0:1].to_broadcast([P, HT, e]),
                                      ALU.subtract).then_inc(exp_in, 1)
                    if n < 4:
                        dve.tensor_copy(to_replace[:, :, 0:K0], top8[:, :, 0:K0])
                        step(dve.memset(to_replace[:, :, K0:8], BIG))
                elif name == "route_keep":
                    dve.wait_ge(exp_out, 2 * n + 1)
                    step(dve.tensor_reduce(esum[:, :], exp8[:, :, :], AX.X, ALU.add))
                    step(dve.reciprocal(erec[:, :], esum[:, :]))
                    step(dve.tensor_tensor(exp8[:, :, :], exp8[:, :, :], bc(erec[:, :], 8), ALU.mult))
                    dve.memset(active[:, :, 0:1], 1.0)
                    for i in range(HT):
                        ins = dve.tensor_tensor_scan(cum8[:, i, :], ones8[:, :], exp8[:, i, :], 0.0, ALU.mult, ALU.add)
                    step(ins)
                    step(dve.tensor_scalar(active[:, :, 1:8], cum8[:, :, 0:7], KEEP, None, ALU.is_lt))
                    dve.tensor_scalar(inactive[:, :, :], active[:, :, :], -BIG, BIG, ALU.mult, ALU.add)
                    step(dve.tensor_tensor(to_replace[:, :, :], top8[:, :, :], active[:, :, :], ALU.mult))
                    step(dve.tensor_tensor(to_replace[:, :, :], to_replace[:, :, :], inactive[:, :, :], ALU.add))
                elif name == "route_weights":
                    e = E0 if n < 4 else E1
                    for i in range(HT):
                        ins = dve.match_replace(replaced[:, i, 0:e], to_replace[:, i, :], logits[:, i, 0:e], -BIG)
                    step(ins)
                    step(dve.tensor_tensor(picked[:, :, 0:e], replaced[:, :, 0:e], logits[:, :, 0:e], ALU.not_equal))
                    dve.wait_ge(exp_out, 2 * n + 2)
                    step(dve.tensor_tensor(picked[:, :, 0:e], picked[:, :, 0:e], expd[:, :, 0:e], ALU.mult))
                    step(dve.tensor_reduce(esum[:, :], picked[:, :, 0:e], AX.X, ALU.add))
                    step(dve.reciprocal(erec[:, :], esum[:, :]))
                    step(dve.tensor_scalar(erec[:, :], erec[:, :], C_SCALE, None, ALU.mult))
                    if n < 4:
                        dve.tensor_scalar(combine[:, :, E0:E0 + 1], sgate[:, :, :], C_SCALE / 2, C_SCALE / 2,
                                          ALU.mult, ALU.add)
                    step(dve.tensor_tensor(combine[:, :, 0:e], picked[:, :, 0:e], bc(erec[:, :], e), ALU.mult))
                elif name == "route_parts":
                    if n:
                        dve.wait_ge(c_turned, n)
                    for k in range(PARTS):
                        part = cparts[:, :, k * EP:(k + 1) * EP]
                        dve.tensor_copy(part, combine[:, :, :]).then_inc(cparts_ready, 1)
                        dve.wait_ge(cparts_ready, 3 * n + k + 1)
                        if k < PARTS - 1:
                            step(dve.tensor_tensor(combine[:, :, :], combine[:, :, :], part, ALU.subtract))
                elif name == "ffn_add":
                    ffn_add(n)
                    if n == 0:
                        dve.wait_ge(small_loaded, 16 * 5)
                        dve.memset(vaug[:, :, :, HD:HD + 1], 1.0)
                        dve.memset(vaug[:, :, :, VW - 1:VW], 0.0)
                        dve.tensor_scalar(hide16[:, :], tri, 1.0, 60000.0, ALU.subtract, ALU.mult)
                        dve.scalar_tensor_tensor(out=ntau[:, :], in0=tau[:, :], scalar=-1.0, in1=tau[:, :],
                                                 op0=ALU.mult, op1=ALU.min).then_inc(dve_consts, 1)
                    if n == 4:
                        dve.wait_ge(act_consts, 2)
                        dve.tensor_scalar(nega[:, :], nega[:, :], -1.0, None, ALU.mult)
                        for b in range(2):
                            dve.memset(xpad[:, b, :, 0:3], 0.0)
                        dve.tensor_scalar(vec[:, :, TAPS + 4], vec[:, :, TAPS + 4], 0.5, None, ALU.mult)
                        dve.tensor_scalar(vec[:, :, TAPS + 2], vec[:, :, TAPS + 2], 0.5, None, ALU.mult)\
                            .then_inc(dve_consts, 1)
                elif name == "qkv_sum":
                    dve.wait_ge(sq_done, n + 1)
                    dve.tensor_reduce(ss[:, n % 2, :], squares.rearrange("p (h d) -> p h d", d=HD), AX.X, ALU.add)\
                        .then_inc(ss_done, 1)
                elif name == "qkv_norm":
                    dve.wait_ge(ss_done, 2 * n + 2)
                    s = ss[:, :, :].rearrange("p t h -> p (t h)")
                    y, a, m = [newton[:, k, :] for k in range(3)]
                    step(dve.tensor_scalar(a.bitcast(I32), s.bitcast(I32), 1, None, ALU.logical_shift_right))
                    step(dve.tensor_scalar(y.bitcast(I32), a.bitcast(I32), -1.0, float(0x5f3759df), ALU.mult, ALU.add))
                    step(dve.tensor_scalar(m, s, -0.5, None, ALU.mult))
                    for _ in range(3):
                        step(dve.tensor_tensor(a, y, m, ALU.mult))
                        step(dve.tensor_tensor(a, a, y, ALU.mult))
                        step(dve.scalar_tensor_tensor(out=y, in0=a, scalar=1.5, in1=y, op0=ALU.add, op1=ALU.mult))
                    step(dve.tensor_tensor(a, s, y, ALU.mult))
                    step(dve.tensor_scalar(a, a, 1e-8 * W_SCALE, None, ALU.add))
                    r = rnorm[:, n % 2, :]
                    step(dve.reciprocal(r, a))
                    q = r.rearrange("p (t h) -> p t h", t=2)[:, :, 0:HEADS]
                    dve.tensor_scalar(q, q, tau[:, 0:1], None, ALU.mult).then_inc(rnorm_done, 1)
                elif name == "k_lo":
                    dve.wait_ge(qkv_his, n + 1)
                    src = raw[n % 4][:, D:2 * D].rearrange("p (h d) -> p h d", d=HD)\
                        .unsqueeze(2).to_broadcast([P, HEADS, 2, HD])
                    dve.tensor_tensor(k4[:, n % 2, :, 1:4:2, :], src, k4[:, n % 2, :, 0:3:2, :], ALU.subtract)
                    dve.tensor_tensor(vaug[:, n % 4, :, HD + 1:2 * HD + 1],
                                      raw[n % 4][:, 2 * D:3 * D].rearrange("p (h d) -> p h d", d=HD),
                                      vaug[:, n % 4, :, 0:HD], ALU.subtract).then_inc(k_los, 1)
                elif name == "k_copy":
                    dve.wait_ge(qk_turned, n + 1)
                    dve.tensor_copy(k4T[:, n // 2 % 2, :, P * (n % 2):P * (n % 2) + P],
                                    ps[:, S1, :].bitcast(F16).rearrange("p (r n) -> p r n", n=P)).then_inc(k_copied, 1)
                elif name == "o_copy":
                    dve.wait_ge(pv_done, 2 * n + 2)
                    g = n % 4
                    dve.tensor_copy(osum[:, :, 4 * g:4 * g + 4, :],
                                    ps[:, S2, 0:8 * VW].rearrange("p (t h c) -> p t h c", t=2, c=VW))\
                        .then_inc(o_copied, 1)
                elif name == "o_add":
                    dve.wait_ge(o_copied, 4 * n + 4)
                    o = onum
                    dve.tensor_tensor(o, osum[:, :, :, 0:HD + 1], osum[:, :, :, HD + 1:VW], ALU.add).then_inc(o_step, 1)
                    dve.wait_ge(o_step, 4 * n + 1)
                    rec = orec[:, :].rearrange("p (t h) -> p t h", t=2)
                    dve.reciprocal(rec, o[:, :, :, HD]).then_inc(o_step, 1)
                    dve.wait_ge(o_step, 4 * n + 2)
                    dve.tensor_scalar(orec[:, :], orec[:, :], nu[:, 0:1], None, ALU.mult).then_inc(o_step, 1)
                    dve.wait_ge(o_step, 4 * n + 3)
                    dve.tensor_tensor(o[:, :, :, 0:HD], o[:, :, :, 0:HD], rec.unsqueeze(3).to_broadcast([P, 2, HEADS, HD]),
                                      ALU.mult).then_inc(o_step, 1)
                    dve.wait_ge(o_step, 4 * n + 4)
                    xb = x[:, 2 * n:2 * n + 2, :].rearrange("p t (h d) -> p t h d", d=HD)
                    dve.tensor_tensor(xb, xb, o[:, :, :, 0:HD], ALU.add).then_inc(x_added[n // 2], 1)
                elif name == "x_conv":
                    dve.wait_ge(tap0_done, n + 1)
                    cv = conv[:, n % 2, :].rearrange("p (s n) -> p s n", s=2)
                    for k in range(1, TAPS):
                        if k > 1:
                            dve.wait_ge(conv_done, 3 * n + k - 1)
                        dve.scalar_tensor_tensor(out=cv, in0=xpad[:, n % 2, :, k:k + T], scalar=vec[:, n % CC, k:k + 1],
                                                 in1=cv, op0=ALU.mult, op1=ALU.add).then_inc(conv_done, 1)
                elif name == "x_silu":
                    dve.wait_ge(ctanh_done, n + 1)
                    dve.scalar_tensor_tensor(out=xs[:, n % CC, :], in0=ctanh, scalar=1.0, in1=conv[:, n % 2, :],
                                             op0=ALU.add, op1=ALU.mult).then_inc(xs_done, 1)
                elif name == "sp_arg":
                    z = sp[0:SHEADS, 1, :]
                    dve.wait_ge(z_ready, n + 1)
                    step(dve.tensor_scalar(z, ps[0:SHEADS, S2, :], 0.5, dtb[:, 0:1], ALU.mult, ALU.add))
                    dve.scalar_tensor_tensor(out=sp[0:SHEADS, 2, :], in0=z, scalar=-1.0, in1=z,
                                             op0=ALU.mult, op1=ALU.min).then_inc(nabs_done, 1)
                elif name == "sp_one":
                    e, w, t1, t2 = [sp[0:SHEADS, k, :] for k in (3, 4, 6, 7)]
                    dve.wait_ge(e_done, n + 1)
                    dve.tensor_scalar(w, e, 1.0, None, ALU.add).then_inc(one_done, 1)
                    dve.wait_ge(one_done, n + 1)
                    dve.tensor_scalar(t2, e, -0.5, 1.0, ALU.mult, ALU.add)
                    step(dve.scalar_tensor_tensor(out=t1, in0=w, scalar=1.0, in1=e, op0=ALU.subtract, op1=ALU.subtract))
                    step(dve.tensor_tensor(t1, t1, t2, ALU.mult))
                elif name == "sp_dt":
                    z, lw, t1 = [sp[0:SHEADS, k, :] for k in (1, 5, 6)]
                    dve.wait_ge(ln_done, n + 1)
                    step(dve.tensor_tensor(t1, lw, t1, ALU.subtract))
                    dve.scalar_tensor_tensor(out=sp[0:SHEADS, DT, :], in0=z, scalar=0.0, in1=t1,
                                             op0=ALU.max, op1=ALU.add).then_inc(dt_done, 1)
                elif name == "scan":
                    cc = n % CC
                    dve.wait_ge(dt_ready, n + 1)
                    dve.wait_ge(decay_done, n + 1)
                    dve.scalar_tensor_tensor(out=drive, in0=ps[:, S2, :], scalar=vec[:, cc, TAPS + 2:TAPS + 3],
                                             in1=xs[:, cc, :], op0=ALU.mult, op1=ALU.mult).then_inc(drive_done, 1)
                    dve.wait_ge(drive_done, n + 1)
                    for q in range(2):
                        ins = dve.tensor_tensor_scan(states[:, q * T:(q + 1) * T], decay[:, q * T:(q + 1) * T],
                                                     drive[:, q * T:(q + 1) * T], 0.0, ALU.mult, ALU.add)
                    ins.then_inc(scan_done, 1)
                elif name == "y":
                    cc = n % CC
                    dve.wait_ge(scan_done, n + 1)
                    dve.wait_ge(skip_done, n + 1)
                    dve.scalar_tensor_tensor(out=states, in0=states, scalar=vec[:, cc, TAPS + 3:TAPS + 4], in1=skip,
                                             op0=ALU.mult, op1=ALU.add).then_inc(y_done, 1)
                    dve.wait_ge(y_done, n + 1)
                    if n:
                        dve.wait_ge(clo_done, n)
                    dve.scalar_tensor_tensor(out=comb, in0=gt[:, cc, :], scalar=1.0, in1=states,
                                             op0=ALU.add, op1=ALU.mult).then_inc(comb_done, 1)
                elif name == "ssm_add":
                    dve.wait_ge(outp_done, CC * (n + 1))
                    add_to_x(S0, n, 0.5 / W_SCALE)

            chunk.eng = dve
            run(chunk, piece)
            ffn_add(PASSES - 1)


def lay_out(i):
    import numpy as np

    f = np.float32
    out = {"x_in": np.ascontiguousarray(i["L0_attn_x"]).reshape(B * T, D)}

    def chunks(gate, up, down, n):
        res = np.zeros((n, P, CW), f)
        for part, w in ((0, gate), (1, up)):
            res[:, :, part * D:(part + 1) * D] = \
                w.reshape(KC, P, n, P).transpose(2, 1, 0, 3).reshape(n, P, KC * P)
        res[:, :, 2 * D:] = down.reshape(n, P, D)
        return res

    def per_partition(w):
        return w.reshape(KC, P, -1).transpose(1, 0, 2).reshape(P, -1, CW).transpose(1, 0, 2)

    gu, dn = i["L0_ffn_expert_gate_up"], i["L0_ffn_expert_down"]
    sgu, sdn = i["L0_ffn_shared_gate_up"], i["L0_ffn_shared_down"]
    gate, up = np.zeros((D, NCH0 * P), f), np.zeros((D, NCH0 * P), f)
    down = np.zeros((NCH0 * P, D), f)
    ne = E0 * I0
    gate[:, :ne] = gu[:, :I0].reshape(ne, D).T
    up[:, :ne] = gu[:, I0:].reshape(ne, D).T
    down[:ne] = dn.transpose(0, 2, 1).reshape(ne, D)
    gate[:, ne:ne + SI0] = sgu[:SI0].T
    up[:, ne:ne + SI0] = sgu[SI0:].T
    down[ne:ne + SI0] = sdn.T
    wqkv = np.concatenate([i["L0_attn_wq"].T, i["L0_attn_wk"].T, i["L0_attn_wv"].T], axis=1)
    out["w0_in"] = np.concatenate([chunks(gate, up, down, NCH0), per_partition(wqkv)])

    gu, dn = i["L1_ffn_gate_up_proj"], i["L1_ffn_down_proj"]
    ne = E1 * I1
    fill = chunks(gu[:, :I1].reshape(ne, D).T, gu[:, I1:].reshape(ne, D).T,
                  dn.transpose(0, 2, 1).reshape(ne, D), NCH1)
    wsg = np.concatenate([i["L1_attn_in_proj_w"].T, i["L1_attn_gate_proj_w"].T], axis=1)
    both = [w.reshape(-1, P, w.shape[1]).transpose(1, 0, 2).reshape(P, -1) for w in (wsg, i["L1_attn_out_proj_w"].T)]
    both = np.concatenate(both, axis=1)
    out["w1_in"] = np.concatenate([fill, both.reshape(P, -1, CW).transpose(1, 0, 2)])

    rw = np.zeros((2, D, EP), f)
    rw[0, :, :E0] = i["L0_ffn_gate_w"].T
    rw[0, :, E0] = i["L0_ffn_shared_gate_vec"][0]
    rw[1, :, :E1] = i["L1_ffn_gate_weight"].T
    out["rw_in"] = np.ascontiguousarray(rw.reshape(2, KC, P, EP).transpose(2, 0, 1, 3).reshape(P, -1))

    row0 = np.arange(NCH0 * P)
    expert0 = np.where(row0 < E0 * I0, row0 // I0, np.where(row0 < E0 * I0 + SI0, E0, -1))
    expert1 = np.arange(NCH1 * P) // I1
    for n, e in ((0, expert0), (1, expert1)):
        out[f"sel{n}_in"] = np.tile(e[None, :] == np.arange(EP)[:, None], (PARTS, 1)).astype(np.float16)
    out["const_in"] = np.concatenate([np.eye(P, dtype=f), np.triu(np.ones((P, P), f))], axis=1)
    out["tau_in"], out["nu_in"] = i["L0_attn_tau"], i["L0_attn_nu"]

    flat = [i["L1_attn_" + k].reshape(INNER) for k in ("conv_b", "A_log", "Bp", "Cp", "Dp")]
    vec = np.concatenate([i["L1_attn_conv_w"], np.stack(flat, axis=1)], axis=1)
    out["vec_in"] = np.ascontiguousarray(vec.reshape(CC, P, NV).transpose(1, 0, 2))
    hd = INNER // SHEADS
    dtw = np.zeros((INNER, SHEADS), f)
    dtw[np.arange(INNER), np.arange(INNER) // hd] = i["L1_attn_dt_w"].reshape(-1)
    out["dtw_in"] = np.ascontiguousarray(dtw.reshape(CC, P, SHEADS).transpose(1, 0, 2))
    out["dtb_in"] = i["L1_attn_dt_b"].reshape(SHEADS, 1)
    out["head_in"] = (np.arange(SHEADS)[:, None] == np.arange(INNER)[None, :] // hd).astype(f).reshape(SHEADS, CC, P)
    return {k: np.ascontiguousarray(v) for k, v in out.items()}


_ORDER = ["x_in", "w0_in", "w1_in", "rw_in", "sel0_in", "sel1_in", "const_in", "tau_in", "nu_in", "vec_in",
          "dtw_in", "dtb_in", "head_in"]


def kernel(**inputs):
    import numpy as _np
    import concourse.bacc as _bacc
    from concourse import mybir as _mybir
    from concourse.bass_utils import run_bass_kernel_spmd as _run

    arrays = lay_out({k: _np.asarray(v) for k, v in inputs.items()})
    nc = _bacc.Bacc("TRN2", target_bir_lowering=False, num_devices=1)
    args = [nc.dram_tensor(n, arrays[n].shape, _mybir.dt.from_np(arrays[n].dtype), kind="ExternalInput").ap()
            for n in _ORDER]
    args.append(nc.dram_tensor("out", (B * T, D), _mybir.dt.float32, kind="ExternalOutput").ap())
    build(nc, *args)
    r = _run(nc, [arrays], core_ids=[0])
    return r.results[0]["out"].reshape(B, T, D)
```
